# Optimizing a Trainium2 kernel written in Bass

```python
import numpy as np
import jax
import jax.numpy as jnp

def _softmax(x, axis=-1):
    return jax.nn.softmax(x, axis=axis)

def _gelu(x):
    return jax.nn.gelu(x, approximate=True)

def _silu(x):
    return jax.nn.silu(x)

def _sigmoid(x):
    return jax.nn.sigmoid(x)

def _layernorm(x, axis=-1, eps=1e-05):
    m = jnp.mean(x, axis=axis, keepdims=True)
    v = jnp.var(x, axis=axis, keepdims=True)
    return (x - m) / jnp.sqrt(v + eps)

def _scatter_add(tgt, idx, src, axis=0):
    return tgt.at[idx].add(src)

def _segment_sum(src, seg, n):
    return jax.ops.segment_sum(src, seg, n)
kernel_name = 'mk_adaln_attn_ffn_d1_seqx_r8_564cf1'

def setup_inputs(seed: int=0):
    np.random.seed(seed)
    _w = jnp.asarray

    def _rec_inputs():
        import jax
        import jax.numpy as jnp
        _rk = jax.random.key(seed)
        x = -0.000125 + 0.9999 * jax.random.normal(jax.random.fold_in(_rk, 1), (64, 32, 512), jnp.float32)
        _lenS = 32 - jax.random.randint(jax.random.fold_in(_rk, 7), (64,), 0, max(1, 32 // 4) + 1, jnp.int32)
        _lenS2 = 32 - jax.random.randint(jax.random.fold_in(_rk, 8), (64,), 0, max(1, 32 // 4) + 1, jnp.int32)
        cond_128 = 0.0061147 + 1.02565 * jax.random.normal(jax.random.fold_in(_rk, 11), (64, 128), jnp.float32)
        fside_S_0 = -0.022604 + 0.987366 * jax.random.normal(jax.random.fold_in(_rk, 12), (32,), jnp.float32)
        return (x, cond_128, fside_S_0)
    x, cond_128, fside_S_0 = _rec_inputs()

    def _L0_cond_setup():
        import jax, jax.numpy as jnp
        import numpy as np
        from jax import lax
        N, C_IN, L = (32, 32, 512)
        C_OUT, K, GROUPS = (32, 9, 4)
        C_DIM, PAD, STRIDE = (128, 4, 1)
        key = jax.random.key(seed)
        k1, k2, k3, k4, k5 = jax.random.split(key, 5)
        x = jax.random.normal(k1, (N, C_IN, L), dtype=jnp.float32)
        c = jax.random.normal(k2, (N, C_DIM), dtype=jnp.float32)
        weight = jax.random.normal(k3, (C_OUT, C_IN // GROUPS, K), dtype=jnp.float32)
        c_weight = jax.random.normal(k4, (C_OUT, C_DIM), dtype=jnp.float32)
        bias = jax.random.normal(k5, (C_OUT,), dtype=jnp.float32)
        return {'x': x, 'c': c, 'weight': weight, 'c_weight': c_weight, 'bias': bias}
    _L0_cond_all = _L0_cond_setup()
    _L0_cond_in = {k: v for k, v in _L0_cond_all.items() if k in ('weight', 'c_weight')}
    del _L0_cond_all

    def _L0_attn_setup():
        import jax, jax.numpy as jnp
        import numpy as np
        import math
        B, S, H = (1, 256, 512)
        NH, NKV, HD = (32, 8, 128)
        GS = 128
        WBITS = 4
        ZERO = float(2 ** (WBITS - 1))
        THETA = 10000.0

        def _dequant_matmul(x, qw, scales):
            w = (qw.astype(jnp.float32) - ZERO) * jnp.repeat(scales, GS, axis=0)
            return x @ w

        def _rope_tables(seq_len, dtype):
            inv_freq = 1.0 / THETA ** (jnp.arange(0, HD, 2, dtype=jnp.float32) / HD)
            freqs = jnp.arange(seq_len, dtype=jnp.float32)[:, None] * inv_freq
            emb = jnp.concatenate([freqs, freqs], axis=-1)
            return (jnp.cos(emb).astype(dtype), jnp.sin(emb).astype(dtype))

        def _rotate_half(x):
            x1, x2 = jnp.split(x, 2, axis=-1)
            return jnp.concatenate([-x2, x1], axis=-1)

        def _apply_rope(x, cos, sin):
            return x * cos[None, None] + _rotate_half(x) * sin[None, None]
        key = jax.random.key(seed)
        ks = jax.random.split(key, 9)
        small = lambda k, shp: jax.random.uniform(k, shp, jnp.float32) * 0.01 + 0.001
        return {'hidden_states': jax.random.normal(ks[0], (B, S, H), jnp.float32), 'scales_q': small(ks[1], (H // GS, NH * HD)), 'scales_k': small(ks[2], (H // GS, NKV * HD)), 'scales_v': small(ks[3], (H // GS, NKV * HD)), 'scales_o': small(ks[4], (NH * HD // GS, H)), 'qw_q': jax.random.randint(ks[5], (H, NH * HD), 0, 2 ** WBITS, jnp.int32), 'qw_k': jax.random.randint(ks[6], (H, NKV * HD), 0, 2 ** WBITS, jnp.int32), 'qw_v': jax.random.randint(ks[7], (H, NKV * HD), 0, 2 ** WBITS, jnp.int32), 'qw_o': jax.random.randint(ks[8], (NH * HD, H), 0, 2 ** WBITS, jnp.int32)}
    _L0_attn_all = _L0_attn_setup()
    _L0_attn_in = {k: v for k, v in _L0_attn_all.items() if k in ('scales_q', 'scales_k', 'scales_v', 'scales_o', 'qw_q', 'qw_k', 'qw_v', 'qw_o')}
    del _L0_attn_all

    def _L0_cond2_setup():
        import jax, jax.numpy as jnp
        import numpy as np
        K = 8
        T = 1.0
        D_EMBD = 128
        IN_C = 32
        OUT_C = 32
        BS = 32
        H = 512
        HID = 128
        key = jax.random.key(seed)
        ks = jax.random.split(key, 10)
        s = lambda fan_in: 1.0 / np.sqrt(fan_in)
        return {'x': jax.random.normal(ks[0], (BS, IN_C, H), dtype=jnp.float32), 'embedding': jax.random.normal(ks[1], (BS, D_EMBD), dtype=jnp.float32), 'W0': jax.random.normal(ks[2], (D_EMBD, HID), dtype=jnp.float32) * s(D_EMBD), 'b0': jnp.zeros((HID,), dtype=jnp.float32), 'W1': jax.random.normal(ks[3], (HID, HID), dtype=jnp.float32) * s(HID), 'b1': jnp.zeros((HID,), dtype=jnp.float32), 'W2': jax.random.normal(ks[4], (HID, K), dtype=jnp.float32) * s(HID), 'b2': jnp.zeros((K,), dtype=jnp.float32), 'weight': jax.random.normal(ks[5], (K, OUT_C, IN_C, 1), dtype=jnp.float32) * s(IN_C), 'bias_k': jax.random.normal(ks[6], (K, OUT_C), dtype=jnp.float32) * 0.1}
    _L0_cond2_all = _L0_cond2_setup()
    _L0_cond2_in = {k: v for k, v in _L0_cond2_all.items() if k in ('W0', 'b0', 'W1', 'b1', 'W2', 'b2', 'weight', 'bias_k')}
    del _L0_cond2_all

    def _L0_ffn_setup():
        import jax, jax.numpy as jnp
        import numpy as np
        B, T, D_IN, D_OUT = (8, 256, 512, 512)
        N_LORAS, RANK = (16, 32)
        SCALING = 1.0
        key = jax.random.key(seed)
        ks = jax.random.split(key, 8)
        std = 1.0 / D_IN ** 0.5
        x = jax.random.normal(ks[0], (B, T, D_IN), dtype=jnp.float32)
        idx = jax.random.randint(ks[1], (B,), 0, N_LORAS)
        gate = jax.nn.one_hot(idx, N_LORAS, dtype=jnp.float32)
        kernel = jax.random.normal(ks[2], (D_IN, D_OUT), dtype=jnp.float32) * std
        bias = jnp.zeros((D_OUT,), dtype=jnp.float32)
        lora_A = jax.random.normal(ks[3], (N_LORAS, RANK, D_IN), dtype=jnp.float32) * std
        lora_B = jax.random.normal(ks[4], (N_LORAS, D_OUT, RANK), dtype=jnp.float32) * 0.01
        lora_A_shared = jax.random.normal(ks[5], (RANK, D_IN), dtype=jnp.float32) * std
        lora_B_shared = jax.random.normal(ks[6], (D_OUT, RANK), dtype=jnp.float32) * 0.01
        return {'x': x, 'gate': gate, 'kernel': kernel, 'bias': bias, 'lora_A': lora_A, 'lora_B': lora_B, 'lora_A_shared': lora_A_shared, 'lora_B_shared': lora_B_shared}
    _L0_ffn_all = _L0_ffn_setup()
    _L0_ffn_in = {k: v for k, v in _L0_ffn_all.items() if k in ('gate', 'kernel', 'bias', 'lora_A', 'lora_B', 'lora_A_shared', 'lora_B_shared')}
    del _L0_ffn_all
    return {'x': x, 'cond_128': cond_128, 'fside_S_0': fside_S_0, 'L0_cond_weight': _L0_cond_in['weight'], 'L0_cond_c_weight': _L0_cond_in['c_weight'], 'L0_attn_scales_q': _L0_attn_in['scales_q'], 'L0_attn_scales_k': _L0_attn_in['scales_k'], 'L0_attn_scales_v': _L0_attn_in['scales_v'], 'L0_attn_scales_o': _L0_attn_in['scales_o'], 'L0_attn_qw_q': _L0_attn_in['qw_q'], 'L0_attn_qw_k': _L0_attn_in['qw_k'], 'L0_attn_qw_v': _L0_attn_in['qw_v'], 'L0_attn_qw_o': _L0_attn_in['qw_o'], 'L0_cond2_W0': _L0_cond2_in['W0'], 'L0_cond2_b0': _L0_cond2_in['b0'], 'L0_cond2_W1': _L0_cond2_in['W1'], 'L0_cond2_b1': _L0_cond2_in['b1'], 'L0_cond2_W2': _L0_cond2_in['W2'], 'L0_cond2_b2': _L0_cond2_in['b2'], 'L0_cond2_weight': _L0_cond2_in['weight'], 'L0_cond2_bias_k': _L0_cond2_in['bias_k'], 'L0_ffn_gate': _L0_ffn_in['gate'], 'L0_ffn_kernel': _L0_ffn_in['kernel'], 'L0_ffn_bias': _L0_ffn_in['bias'], 'L0_ffn_lora_A': _L0_ffn_in['lora_A'], 'L0_ffn_lora_B': _L0_ffn_in['lora_B'], 'L0_ffn_lora_A_shared': _L0_ffn_in['lora_A_shared'], 'L0_ffn_lora_B_shared': _L0_ffn_in['lora_B_shared']}

def reference(x, cond_128, fside_S_0, L0_cond_weight, L0_cond_c_weight, L0_attn_scales_q, L0_attn_scales_k, L0_attn_scales_v, L0_attn_scales_o, L0_attn_qw_q, L0_attn_qw_k, L0_attn_qw_v, L0_attn_qw_o, L0_cond2_W0, L0_cond2_b0, L0_cond2_W1, L0_cond2_b1, L0_cond2_W2, L0_cond2_b2, L0_cond2_weight, L0_cond2_bias_k, L0_ffn_gate, L0_ffn_kernel, L0_ffn_bias, L0_ffn_lora_A, L0_ffn_lora_B, L0_ffn_lora_A_shared, L0_ffn_lora_B_shared):
    import jax
    import jax.numpy as jnp

    def _L0_cond_ref(x, c, weight, c_weight, bias):
        import jax, jax.numpy as jnp
        import numpy as np
        from jax import lax
        N, C_IN, L = (32, 32, 512)
        C_OUT, K, GROUPS = (32, 9, 4)
        C_DIM, PAD, STRIDE = (128, 4, 1)
        out = lax.conv_general_dilated(x, weight, window_strides=(STRIDE,), padding=[(PAD, PAD)], dimension_numbers=('NCH', 'OIH', 'NCH'), feature_group_count=GROUPS)
        ctx = jnp.einsum('nd,od->no', c, c_weight)
        out = out + ctx[:, :, None] + bias[None, :, None]
        return out

    def _L0_attn_ref(hidden_states, scales_q, scales_k, scales_v, scales_o, qw_q, qw_k, qw_v, qw_o):
        import jax, jax.numpy as jnp
        import numpy as np
        import math
        B, S, H = (1, 256, 512)
        NH, NKV, HD = (32, 8, 128)
        GS = 128
        WBITS = 4
        ZERO = float(2 ** (WBITS - 1))
        THETA = 10000.0

        def _dequant_matmul(x, qw, scales):
            w = (qw.astype(jnp.float32) - ZERO) * jnp.repeat(scales, GS, axis=0)
            return x @ w

        def _rope_tables(seq_len, dtype):
            inv_freq = 1.0 / THETA ** (jnp.arange(0, HD, 2, dtype=jnp.float32) / HD)
            freqs = jnp.arange(seq_len, dtype=jnp.float32)[:, None] * inv_freq
            emb = jnp.concatenate([freqs, freqs], axis=-1)
            return (jnp.cos(emb).astype(dtype), jnp.sin(emb).astype(dtype))

        def _rotate_half(x):
            x1, x2 = jnp.split(x, 2, axis=-1)
            return jnp.concatenate([-x2, x1], axis=-1)

        def _apply_rope(x, cos, sin):
            return x * cos[None, None] + _rotate_half(x) * sin[None, None]
        b, s, _ = hidden_states.shape
        q = _dequant_matmul(hidden_states, qw_q, scales_q).reshape(b, s, NH, HD).transpose(0, 2, 1, 3)
        k = _dequant_matmul(hidden_states, qw_k, scales_k).reshape(b, s, NKV, HD).transpose(0, 2, 1, 3)
        v = _dequant_matmul(hidden_states, qw_v, scales_v).reshape(b, s, NKV, HD).transpose(0, 2, 1, 3)
        cos, sin = _rope_tables(s, hidden_states.dtype)
        q = _apply_rope(q, cos, sin)
        k = _apply_rope(k, cos, sin)
        rep = NH // NKV
        k = jnp.repeat(k, rep, axis=1)
        v = jnp.repeat(v, rep, axis=1)
        scores = jnp.einsum('bhqd,bhkd->bhqk', q, k) / math.sqrt(HD)
        causal = jnp.tril(jnp.ones((s, s), dtype=bool))
        scores = jnp.where(causal[None, None], scores, jnp.finfo(scores.dtype).min)
        attn = jax.nn.softmax(scores.astype(jnp.float32), axis=-1).astype(q.dtype)
        ctx = jnp.einsum('bhqk,bhkd->bhqd', attn, v)
        ctx = ctx.transpose(0, 2, 1, 3).reshape(b, s, NH * HD)
        return _dequant_matmul(ctx, qw_o, scales_o)

    def _L0_cond2_ref(x, embedding, W0, b0, W1, b1, W2, b2, weight, bias_k):
        import jax, jax.numpy as jnp
        import numpy as np
        K = 8
        T = 1.0
        D_EMBD = 128
        IN_C = 32
        OUT_C = 32
        BS = 32
        H = 512
        HID = 128
        h = jax.nn.gelu(embedding @ W0 + b0, approximate=False)
        h = jax.nn.gelu(h @ W1 + b1, approximate=False)
        att = jax.nn.softmax((h @ W2 + b2) / T, axis=-1)
        agg_w = jnp.einsum('bk,koi->boi', att, weight[..., 0])
        agg_b = att @ bias_k
        out = jnp.einsum('boi,bih->boh', agg_w, x) + agg_b[:, :, None]
        return out

    def _L0_ffn_ref(x, gate, kernel, bias, lora_A, lora_B, lora_A_shared, lora_B_shared):
        import jax, jax.numpy as jnp
        import numpy as np
        B, T, D_IN, D_OUT = (8, 256, 512, 512)
        N_LORAS, RANK = (16, 32)
        SCALING = 1.0
        base_out = jnp.matmul(x, kernel) + bias
        b = gate.shape[0]
        x_flat = x.reshape(b, -1, x.shape[-1])
        A_eff = jnp.einsum('bn,nri->bri', gate, lora_A)
        B_eff = jnp.einsum('bn,nor->bor', gate, lora_B)
        Ax = jnp.einsum('bri,bti->btr', A_eff, x_flat)
        delta_flat = jnp.einsum('bor,btr->bto', B_eff, Ax)
        Ax_s = jnp.einsum('ri,bti->btr', lora_A_shared, x_flat)
        delta_flat = delta_flat + jnp.einsum('or,btr->bto', lora_B_shared, Ax_s)
        delta = delta_flat.reshape(x.shape[:-1] + (kernel.shape[-1],))
        return base_out + (SCALING * delta).astype(base_out.dtype)
    x = x + _L0_attn_ref(_L0_cond_ref(x, cond_128, L0_cond_weight, L0_cond_c_weight, fside_S_0), L0_attn_scales_q, L0_attn_scales_k, L0_attn_scales_v, L0_attn_scales_o, L0_attn_qw_q, L0_attn_qw_k, L0_attn_qw_v, L0_attn_qw_o)
    x = x + _L0_ffn_ref(_L0_cond2_ref(x, cond_128, L0_cond2_W0, L0_cond2_b0, L0_cond2_W1, L0_cond2_b1, L0_cond2_W2, L0_cond2_b2, L0_cond2_weight, L0_cond2_bias_k), L0_ffn_gate, L0_ffn_kernel, L0_ffn_bias, L0_ffn_lora_A, L0_ffn_lora_B, L0_ffn_lora_A_shared, L0_ffn_lora_B_shared)
    return x

_drawn_inputs = setup_inputs


def setup_inputs(seed=0):
    import zlib

    import numpy as np

    out = dict(_drawn_inputs(seed))
    spreads = {'L0_cond2_b0': (0.0, 0.74),
     'L0_cond2_b1': (0.0, 0.49),
     'L0_cond2_b2': (0.0, 0.1),
     'L0_ffn_bias': (0.0, 0.8)}
    factors = {'L0_cond2_bias_k': 8.0, 'L0_ffn_lora_A_shared': 2.683}
    for name, (base, spread) in spreads.items():
        noise = np.random.default_rng([zlib.crc32(name.encode()), seed]).standard_normal(out[name].shape)
        drawn = base * np.exp(spread * noise) if base else spread * noise
        out[name] = jnp.asarray(drawn.astype(out[name].dtype))
    for name, factor in factors.items():
        out[name] = (out[name] * factor).astype(out[name].dtype)
    return out
```

```python
from contextlib import ExitStack

import concourse.bass as bass
from concourse import mybir

F32 = mybir.dt.float32
F32R = mybir.dt.float32r
I32 = mybir.dt.int32
ALU = mybir.AluOpType
ACT = mybir.ActivationFunctionType
AX_X = mybir.AxisListType.X

P = 128
BATCH, SEQ, HID = 64, 32, 512
TOKENS = BATCH * SEQ
TILES = TOKENS // P
BPT = P // SEQ
KT = HID // P
HEAD = 128
KV_HEADS = 8
REP = 4
BLOCK = 512
TPB = BLOCK // P
BPB = BLOCK // SEQ
BLOCKS = TOKENS // BLOCK
STEPS = KV_HEADS * BLOCKS
TAPS, PAD = 9, 4
XW = HID + 2 * PAD
MIX = 8
NLORA, RANK = 16, 32
LGROUPS = 8
ZERO_POINT = 8.0

C_K, C_Q, C_V, C_O = 0, 1, 5, 6
CHUNKS = 10
QKV = 6

COS, SIN, LIM, IDN, BD8, BD32, ID32, CON_N = 0, 32, 64, 96, 224, 240, 244, 276


def build(nc, a, out):
    ctx = ExitStack()
    with ctx:
        def sb(name, shape, dt=F32):
            return ctx.enter_context(nc.sbuf_tensor(name, shape, dt))

        def sem(name):
            return ctx.enter_context(nc.semaphore(name))

        bank = [ctx.enter_context(nc.psum_tensor(f"bank{i}", [P, 512], F32)) for i in range(8)]
        q_bank, k_bank, v_bank, s_bank, t_bank = bank[0:4], bank[4], bank[5], bank[6], bank[7]

        acc = sb("acc", [P, TILES, HID])
        hT_hi = sb("hT_hi", [P, KT * TOKENS], F32R)
        hT_lo = sb("hT_lo", [P, KT * TOKENS], F32R)
        w_hi = sb("w_hi", [P, CHUNKS * 512], F32R)
        w_lo = sb("w_lo", [P, CHUNKS * 512], F32R)
        w32 = sb("w32", [P, CHUNKS * 512])
        w_scale = sb("w_scale", [P, 2, 512])
        ctx_hi = sb("ctx_hi", [P, REP * BLOCK], F32R)
        ctx_lo = sb("ctx_lo", [P, REP * BLOCK], F32R)
        work = sb("work", [P, 5632])
        con = sb("con", [P, CON_N])
        mixw = sb("mixw", [P, TILES, SEQ])
        cbias = sb("cbias", [P, TILES])
        mbias = sb("mbias", [P, TILES])
        stat = sb("stat", [P, 3, BPB])

        roped_q = work[:, 0:2048]
        rope_c = work[:, 2048:2560]
        rope_s = work[:, 2560:3072]
        roped_k = work[:, 3072:3584]
        vT = work[:, 3584:4096]
        v_sb = work[:, 4096:4608]
        prob = work[:, 4608:5120]
        probT = work[:, 5120:5632]

        cosT, sinT, limit = con[:, COS:COS + 32], con[:, SIN:SIN + 32], con[:, LIM:LIM + 32]
        ident = con[:, IDN:IDN + 128]

        h_tile = [work[:, 512 * s:512 * s + 512] for s in range(2)]
        o = 1024
        su = {}
        for name, rows, n in (("t72", P, TAPS * 8), ("condT", P, BATCH), ("w0", P, 128), ("w1", P, 128),
                              ("w2", P, MIX), ("cwT", P, 128), ("b0", P, 1), ("b1", P, 1), ("fb", P, 1),
                              ("b2", BATCH, MIX), ("biask", MIX, 128), ("sel", MIX, MIX * 128),
                              ("mixk", P, MIX * 32), ("h1", P, BATCH), ("h2", P, BATCH), ("att", BATCH, MIX),
                              ("attT", MIX, BATCH), ("attR", P, MIX * TILES), ("prod", P, 512)):
            su[name] = work[0:rows, o:o + n]
            o += n
        convw = work[:, o:o + TAPS * 128]
        assert o + TAPS * 128 <= 5632
        CW = C_O * 512
        convw_hi = w_hi[:, CW:CW + TAPS * 128]
        convw_lo = w_lo[:, CW:CW + TAPS * 128]
        x_hi = [ctx_hi[:, s * XW:(s + 1) * XW] for s in range(2)]
        x_lo = [ctx_lo[:, s * XW:(s + 1) * XW] for s in range(2)]

        FK, FB, FY, FX = 0, 2048, 6144, 7168
        loraA = w32[:, 0:2048]
        loraB = w32[:, 2048:4096]
        gateT = w32[:, 4096:4128]
        sharedA = w32[:, 4128:4256]
        sharedB = w32[32:64, 4256:4768]
        kern = work[:, 0:2048]
        gsel = work[:, 2048:3072]
        y_sb = [work[:, 3072 + 512 * s:3584 + 512 * s] for s in range(2)]
        ax_sb = [work[:, 4096 + 128 * s:4224 + 128 * s] for s in range(2)]
        mixbd = [work[:, 4608 + 128 * s:4736 + 128 * s] for s in range(2)]

        con_in, set_in = sem("con_in"), sem("set_in")
        x_in = [sem(f"x_in{i}") for i in range(4)]
        su_pe, su_act, su_dve = sem("su_pe"), sem("su_act"), sem("su_dve")
        cbias_ok, convw_ok, setup_read = sem("cbias_ok"), sem("convw_ok"), sem("setup_read")
        pads, x_hi_ok, x_split = sem("pads"), sem("x_hi_ok"), sem("x_split")
        conv_done, h_ok, ht_done, hT_hi_ok, hT_ok = (sem(n) for n in
                                                     ("conv_done", "h_ok", "ht_done", "hT_hi_ok", "hT_ok"))
        w_in = [sem(f"w_in{c}") for c in range(CHUNKS)]
        scale_in = [sem(f"scale_in{s}") for s in range(2)]
        w_zeroed, w_scaled, w_hi_ok, w_ready = (sem(n) for n in ("w_zeroed", "w_scaled", "w_hi_ok", "w_ready"))
        proj_done, rope_part, roped, vT_ok = (sem(n) for n in ("proj_done", "rope_part", "roped", "vT_ok"))
        vt_done, v_ok, scores_done, s_read = (sem(n) for n in ("vt_done", "v_ok", "scores_done", "s_read"))
        sm_step, exp_done, prob_ok = sem("sm_step"), sem("exp_done"), sem("prob_ok")
        pt_done, probT_ok, pv_done = sem("pt_done"), sem("probT_ok"), sem("pv_done")
        ctx_hi_ok, ctx_ok, out_done, out_added = (sem(n) for n in ("ctx_hi_ok", "ctx_ok", "out_done", "out_added"))
        lora_in, kern_in, gsel_ok = sem("lora_in"), sem("kern_in"), sem("gsel_ok")
        lora_pe, lora_hi, lora_ok = sem("lora_pe"), sem("lora_hi"), sem("lora_ok")
        kern_hi, kern_ok, rest_ok = sem("kern_hi"), sem("kern_ok"), sem("rest_ok")
        bd_ok, y_done, y_ok, yt_done, yT_hi_ok, yT_ok = (sem(n) for n in
                                                         ("bd_ok", "y_done", "y_ok", "yt_done", "yT_hi_ok", "yT_ok"))
        ax_done, ax_ok, axt_done, axT_hi_ok, axT_ok = (sem(n) for n in
                                                       ("ax_done", "ax_ok", "axt_done", "axT_hi_ok", "axT_ok"))
        ffn_done, result, stored = sem("ffn_done"), sem("result"), sem("stored")

        SET_LOADS = 15
        LORA_LOADS = 6 + (P // RANK - 1)

        block = ctx.enter_context(nc.Block())

        def f32(ap):
            return ap.bitcast(F32)

        def hT(part, kt, tok0, n):
            return part[:, bass.ds(tok0 + kt * TOKENS, n)]

        def used(eng, signal, count):
            if not isinstance(count, int) or count > 0:
                eng.wait_ge(signal, count)

        def context(part, r):
            return part[:, :].rearrange("p (h t b q) -> p t h b q", h=REP, t=TPB, b=BPT)[:, :, :, r, :]

        def bank_thq(r):
            return q_bank[r][:, :].rearrange("p (t h q) -> p t h q", t=TPB, h=REP)

        @block.sync
        def _(sp):
            sp.dma_start(con[:, :], a["con"]).then_inc(con_in, 16)
            for name in ("condT", "w0", "w1", "w2", "b0", "b1", "biask", "sel"):
                sp.dma_start(su[name], a[name]).then_inc(set_in, 16)
            sp.dma_start(su["b2"], a["b2"].to_broadcast([BATCH, MIX])).then_inc(set_in, 16)
            sp.dma_start(su["cwT"], a["cwT"]).then_inc(set_in, 16)
            sp.dma_start(su["t72"], a["t72"]).then_inc(set_in, 16)
            sp.dma_start(su["fb"], a["fb"]).then_inc(set_in, 16)
            sp.dma_start(su["mixk"], a["mixk"]).then_inc(set_in, 16)

            def load(g, c):
                sp.dma_start(w32[:, c * 512:(c + 1) * 512].bitcast(I32),
                             a["qw"][g, c, :, :]).then_inc(w_in[c], 16)

            def load_scale(g, c):
                sp.dma_start(w_scale[:, c % 2, :],
                             a["scales"][g, c:c + 1, :].to_broadcast([P, 512])).then_inc(scale_in[c % 2], 16)

            for c in range(CHUNKS):
                load(0, c)
                if c >= 2:
                    sp.wait_ge(w_scaled, c - 1)
                load_scale(0, c)
            with sp.Fori(1, KV_HEADS) as g:
                for c in range(CHUNKS):
                    sp.wait_ge(w_ready, (g - 1) * CHUNKS + c + 1)
                    load(g, c)
                    sp.wait_ge(w_scaled, g * CHUNKS + c - 1)
                    load_scale(g, c)
            sp.wait_ge(w_ready, KV_HEADS * CHUNKS)
            sp.dma_start(loraA.rearrange("p (t n) -> p t n", t=4), a["loraA"]).then_inc(lora_in, 16)
            sp.dma_start(loraB.rearrange("p (t n) -> p t n", t=4), a["loraB"]).then_inc(lora_in, 16)
            for q in range(P // RANK):
                sp.dma_start(gateT[q * RANK:(q + 1) * RANK, :],
                             a["gateT"][q:q + 1, :].to_broadcast([RANK, 32])).then_inc(lora_in, 16)
            sp.dma_start(sharedA, a["sharedA"]).then_inc(lora_in, 16)
            sp.dma_start(sharedB, a["sharedB"]).then_inc(lora_in, 16)
            sp.dma_start(w_scale[2 * RANK:2 * RANK + 1, 0, :], a["fbias"]).then_inc(lora_in, 16)
            sp.wait_ge(scores_done, STEPS)
            sp.dma_start(kern.rearrange("p (t n) -> p t n", t=KT), a["kern"]).then_inc(kern_in, 16)
            with sp.Fori(0, TILES // 2) as i:
                sp.wait_ge(result, 2 * i + 2)
                sp.dma_start(out[bass.ds(i, 1), :, :, :].rearrange("a p t n -> (a p) t n"),
                             acc[:, bass.ds(2 * i, 2), :]).then_inc(stored, 16)
            sp.wait_ge(stored, 16 * (TILES // 2))

        @block.gpsimd
        def _(pool):
            def scale(g, c):
                w = w32[:, c * 512:(c + 1) * 512]
                pool.wait_ge(w_zeroed, g * CHUNKS + c + 1)
                pool.wait_ge(scale_in[c % 2], 16 * (g * (CHUNKS // 2) + c // 2 + 1))
                nc.gpsimd.tensor_tensor(w, w, w_scale[:, c % 2, :], ALU.mult).then_inc(w_scaled, 1)

            def low(g, c):
                sl = slice(c * 512, (c + 1) * 512)
                pool.wait_ge(w_hi_ok, g * CHUNKS + c + 1)
                nc.gpsimd.tensor_tensor(w_lo[:, sl], w32[:, sl], f32(w_hi[:, sl]), ALU.subtract).then_inc(w_ready, 1)

            with pool.Fori(0, KV_HEADS) as g:
                for c in range(CHUNKS):
                    scale(g, c)
                for c in range(CHUNKS):
                    low(g, c)
            pool.wait_ge(kern_in, 16)
            pool.wait_ge(proj_done, STEPS * QKV)
            nc.gpsimd.tensor_copy(hT_hi[:, FK:FK + 2048], kern).then_inc(kern_hi, 1)
            pool.wait_ge(kern_hi, 1)
            nc.gpsimd.tensor_tensor(hT_lo[:, FK:FK + 2048], kern, f32(hT_hi[:, FK:FK + 2048]),
                                    ALU.subtract).then_inc(kern_ok, 1)

            def block_diagonal(t, s):
                nc.gpsimd.tensor_tensor(
                    mixbd[s].rearrange("p (b o) -> p b o", b=BPT),
                    mixw[:, bass.ds(t, 1), :].to_broadcast([P, BPT, SEQ]),
                    con[:, BD32:BD32 + BPT].rearrange("p (b o) -> p b o", o=1).to_broadcast([P, BPT, SEQ]),
                    ALU.mult).then_inc(bd_ok, 1)

            rest = slice(2 * RANK, P)
            pool.wait_ge(kern_ok, 1)
            nc.gpsimd.memset(f32(hT_hi[rest, FB:FB + 4096]), 0.0).then_inc(rest_ok, 1)
            nc.gpsimd.memset(f32(hT_lo[rest, FB:FB + 4096]), 0.0).then_inc(rest_ok, 1)
            pool.wait_ge(rest_ok, 2)
            pool.wait_ge(pv_done, STEPS)
            for s in range(2):
                nc.gpsimd.memset(ax_sb[s][:, 2 * RANK:P], 0.0).then_inc(rest_ok, 1)
            pool.wait_ge(rest_ok, 4)
            for s in range(2):
                nc.gpsimd.memset(ax_sb[s][:, 2 * RANK:2 * RANK + 1], 1.0).then_inc(rest_ok, 1)

            pool.wait_ge(pt_done, STEPS)
            for s in range(2):
                block_diagonal(s, s)
            with pool.Fori(1, TILES // 2) as i:
                for s in range(2):
                    pool.wait_ge(y_done, 2 * i + s - 1)
                    block_diagonal(2 * i + s, s)

        @block.scalar
        def _(act):
            for q in range(4):
                act.dma_start(acc[:, 4 * q:4 * q + 4, :],
                              a["x"][4 * q:4 * q + 4, :, :].rearrange("t p n -> p t n")).then_inc(x_in[q], 16)
            act.wait_ge(su_pe, 2)
            nc.scalar.activation(su["h1"], t_bank[:, 64:128], ACT.Gelu, bias=su["b0"]).then_inc(su_act, 1)
            act.wait_ge(su_pe, 3)
            nc.scalar.activation(su["h2"], s_bank[:, 128:192], ACT.Gelu, bias=su["b1"]).then_inc(su_act, 1)
            act.wait_ge(su_dve, 3)
            nc.scalar.activation(su["att"], su["att"], ACT.Exp).then_inc(su_act, 1)

            def zero_point(g, c):
                w = w32[:, c * 512:(c + 1) * 512]
                act.wait_ge(w_in[c], 16 * (g + 1))
                nc.scalar.activation(w, w.bitcast(I32), ACT.Copy, bias=-ZERO_POINT).then_inc(w_zeroed, 1)

            def high(g, c):
                sl = slice(c * 512, (c + 1) * 512)
                act.wait_ge(w_scaled, g * CHUNKS + c + 1)
                nc.scalar.activation(w_hi[:, sl], w32[:, sl], ACT.Identity).then_inc(w_hi_ok, 1)

            def conv_pair(i):
                for s in range(2):
                    act.wait_ge(conv_done, 2 * i + s + 1)
                    act.wait_ge(cbias_ok, 4)
                    used(act, ht_done, 2 * i)
                    nc.scalar.activation(h_tile[s], q_bank[s][:, :], ACT.Identity,
                                         bias=cbias[:, bass.ds(2 * i + s, 1)]).then_inc(h_ok, 1)
                for s in range(2):
                    act.wait_ge(ht_done, 2 * i + s + 1)
                    nc.scalar.activation(
                        hT_hi[:, :].rearrange("p (k t n) -> p k t n", k=KT, n=P)[:, :, bass.ds(2 * i + s, 1), :],
                        q_bank[2 + s][:, :].rearrange("p (k t n) -> p k t n", k=KT, t=1), ACT.Identity).then_inc(hT_hi_ok, 1)

            conv_pair(0)
            with act.Fori(1, TILES // 4) as i:
                conv_pair(i)
            for c in range(CHUNKS):
                zero_point(0, c)
            for c in range(QKV):
                high(0, c)
            with act.Fori(TILES // 4, TILES // 2) as i:
                conv_pair(i)
            for c in range(QKV, CHUNKS):
                high(0, c)

            def copy_vT(n):
                act.wait_ge(proj_done, n * QKV + QKV)
                used(act, vt_done, n)
                nc.scalar.activation(vT, v_bank[:, :], ACT.Identity).then_inc(vT_ok, 1)

            def copy_v(n):
                act.wait_ge(vt_done, n + 1)
                used(act, pv_done, n)
                nc.scalar.activation(v_sb, t_bank[:, :], ACT.Identity).then_inc(v_ok, 1)

            def exps(n):
                act.wait_ge(sm_step, 5 * n + 2)
                nc.scalar.activation(prob, prob, ACT.Exp, scale=HEAD ** -0.5).then_inc(exp_done, 1)

            def copy_probT(n):
                act.wait_ge(pt_done, n + 1)
                used(act, pv_done, n)
                nc.scalar.activation(probT, t_bank[:, :], ACT.Identity).then_inc(probT_ok, 1)

            def context_hi(n):
                act.wait_ge(pv_done, n + 1)
                used(act, out_done, TPB * n)
                for r in range(BPT):
                    nc.scalar.activation(context(ctx_hi, r), bank_thq(r), ACT.Identity).then_inc(ctx_hi_ok, 1)

            copy_vT(0)
            copy_v(0)
            exps(0)

            def body(n):
                copy_probT(n)
                copy_vT(n + 1)
                context_hi(n)
                copy_v(n + 1)
                exps(n + 1)

            def group(g):
                body(g * BLOCKS)
                for c in range(CHUNKS // 2):
                    zero_point(g + 1, c)
                body(g * BLOCKS + 1)
                for c in range(CHUNKS // 2, CHUNKS):
                    zero_point(g + 1, c)
                body(g * BLOCKS + 2)
                for c in range(QKV):
                    act.wait_ge(proj_done, (g * BLOCKS + 3) * QKV + c + 1)
                    high(g + 1, c)
                body(g * BLOCKS + 3)
                act.wait_ge(out_done, (g + 1) * BLOCKS * TPB)
                for c in range(QKV, CHUNKS):
                    high(g + 1, c)

            group(0)
            with act.Fori(1, KV_HEADS - 1) as g:
                group(g)
            with act.Fori((KV_HEADS - 1) * BLOCKS, STEPS - 1) as n:
                body(n)
            copy_probT(STEPS - 1)
            context_hi(STEPS - 1)

            catA = w_hi[:, 0:2048].rearrange("p (k g r) -> p k g r", k=KT, g=LGROUPS)
            act.wait_ge(lora_pe, 1)
            for k in range(KT):
                src = (s_bank, t_bank)[k // 2][:, 256 * (k % 2):256 * (k % 2) + 256]
                nc.scalar.activation(catA[:, k, :, 0:RANK], src.rearrange("p (g r) -> p g r", g=LGROUPS),
                                     ACT.Identity).then_inc(lora_hi, 1)
            act.wait_ge(lora_in, 16 * LORA_LOADS)
            for k in range(KT):
                nc.scalar.activation(
                    catA[:, k, :, RANK:2 * RANK],
                    sharedA[:, k * RANK:(k + 1) * RANK].rearrange("p (g r) -> p g r", g=1).to_broadcast([P, LGROUPS, RANK]),
                    ACT.Identity).then_inc(lora_hi, 1)
            for j in range(2):
                act.wait_ge(lora_pe, 2 + j)
                for b in range(4):
                    g = 4 * j + b
                    nc.scalar.activation(hT_hi[0:RANK, FB + g * 512:FB + (g + 1) * 512],
                                         q_bank[j][b * RANK:(b + 1) * RANK, :], ACT.Identity).then_inc(lora_hi, 1)
            for g in range(LGROUPS):
                nc.scalar.activation(hT_hi[RANK:2 * RANK, FB + g * 512:FB + (g + 1) * 512], sharedB,
                                     ACT.Identity).then_inc(lora_hi, 1)
            act.wait_ge(rest_ok, 2)
            bias_row = w_scale[2 * RANK:2 * RANK + 1, 0, :]
            for g in range(LGROUPS):
                nc.scalar.activation(hT_hi[2 * RANK:2 * RANK + 1, FB + g * 512:FB + (g + 1) * 512], bias_row,
                                     ACT.Identity).then_inc(lora_hi, 1)
            act.wait_ge(lora_ok, 32)

            def feed_forward_pair(i):
                for s in range(2):
                    act.wait_ge(y_done, 2 * i + s + 1)
                    used(act, yt_done, 2 * i)
                    nc.scalar.activation(y_sb[s], q_bank[s][:, :], ACT.Identity,
                                         bias=mbias[:, bass.ds(2 * i + s, 1)]).then_inc(y_ok, 1)
                for s in range(2):
                    act.wait_ge(yt_done, 2 * i + s + 1)
                    used(act, ffn_done, 2 * i)
                    nc.scalar.activation(hT_hi[:, FY + 512 * s:FY + 512 * (s + 1)], q_bank[2 + s][:, :],
                                         ACT.Identity).then_inc(yT_hi_ok, 1)
                for s in range(2):
                    act.wait_ge(ax_done, 2 * i + s + 1)
                    used(act, axt_done, 2 * i)
                    nc.scalar.activation(ax_sb[s][:, 0:2 * RANK], (s_bank, t_bank)[s][:, 0:2 * RANK],
                                         ACT.Identity).then_inc(ax_ok, 1)
                for s in range(2):
                    act.wait_ge(axt_done, 2 * i + s + 1)
                    nc.scalar.activation(hT_hi[:, FX + P * s:FX + P * (s + 1)], (s_bank, t_bank)[s][:, 128:256],
                                         ACT.Identity).then_inc(axT_hi_ok, 1)

            feed_forward_pair(0)
            with act.Fori(1, TILES // 2) as i:
                feed_forward_pair(i)

        @block.vector
        def _(dve):
            dve.wait_ge(con_in, 16)
            dve.wait_ge(set_in, 16 * 13)
            dve.memset(f32(ctx_hi[:, :]), 0.0).then_inc(pads, 1)
            dve.memset(f32(ctx_lo[:, :]), 0.0).then_inc(pads, 1)
            nc.vector.tensor_tensor(
                convw.rearrange("p (k j c) -> p k j c", k=TAPS, c=8),
                su["t72"].rearrange("p (k j c) -> p k j c", k=TAPS, j=1).to_broadcast([P, TAPS, 16, 8]),
                con[:, BD8:BD8 + 16].rearrange("p (k j c) -> p k j c", k=1, c=1).to_broadcast([P, TAPS, 16, 8]),
                ALU.mult).then_inc(convw_ok, 1)
            dve.wait_ge(convw_ok, 1)
            nc.vector.tensor_copy(convw_hi, convw).then_inc(convw_ok, 1)
            dve.wait_ge(convw_ok, 2)
            nc.vector.tensor_tensor(convw_lo, convw, f32(convw_hi), ALU.subtract).then_inc(convw_ok, 1)

            def per_tile(ap, b):
                return ap[b * 32:(b + 1) * 32, :].rearrange("p (t b) -> p t b", b=BPT)[:, :, b]

            dve.wait_ge(su_pe, 1)
            for b in range(BPT):
                nc.vector.tensor_scalar(cbias[b * 32:(b + 1) * 32, :], per_tile(s_bank[:, 0:64], b),
                                        su["fb"][b * 32:(b + 1) * 32, :], None, ALU.add).then_inc(cbias_ok, 1)
            att, st = su["att"], stat[0:BATCH, :, 0:1]
            dve.wait_ge(su_pe, 4)
            nc.vector.tensor_tensor(att, s_bank[0:BATCH, 192:200], su["b2"], ALU.add).then_inc(su_dve, 1)
            dve.wait_ge(su_dve, 1)
            nc.vector.tensor_reduce(st[:, 0, :], att, AX_X, ALU.max).then_inc(su_dve, 1)
            dve.wait_ge(su_dve, 2)
            nc.vector.tensor_scalar(att, att, st[:, 0, :], None, ALU.subtract).then_inc(su_dve, 1)
            dve.wait_ge(su_act, 3)
            nc.vector.tensor_reduce(st[:, 1, :], att, AX_X, ALU.add).then_inc(su_dve, 1)
            dve.wait_ge(su_dve, 4)
            nc.vector.reciprocal(st[:, 2, :], st[:, 1, :]).then_inc(su_dve, 1)
            dve.wait_ge(su_dve, 5)
            nc.vector.tensor_scalar(att, att, st[:, 2, :], None, ALU.mult).then_inc(su_dve, 1)
            dve.wait_ge(su_pe, 5)
            nc.vector.tensor_copy(su["attT"], s_bank[0:MIX, 256:320]).then_inc(su_dve, 1)
            dve.wait_ge(su_pe, 6)
            attR = su["attR"].rearrange("p (k t) -> p k t", k=MIX)
            for b in range(BPT):
                rows = slice(b * 32, (b + 1) * 32)
                nc.vector.tensor_copy(mbias[rows, :], per_tile(s_bank[:, 320:384], b)).then_inc(su_dve, 1)
                nc.vector.tensor_copy(attR[rows, :, :],
                                      t_bank[rows, :].rearrange("p (k t b) -> p k t b", k=MIX, b=BPT)[:, :, :, b])\
                    .then_inc(su_dve, 1)
            mixk = su["mixk"].rearrange("p (k o) -> p k o", k=MIX)
            prod = su["prod"].rearrange("p (t o) -> p t o", t=TILES)
            step = 7 + 2 * BPT
            for k in range(MIX):
                dve.wait_ge(su_dve, step)
                nc.vector.tensor_tensor(mixw[:, :, :] if k == 0 else prod,
                                        attR[:, k, :].rearrange("p (t o) -> p t o", o=1).to_broadcast([P, TILES, SEQ]),
                                        mixk[:, k:k + 1, :].to_broadcast([P, TILES, SEQ]), ALU.mult).then_inc(su_dve, 1)
                step += 1
                if k:
                    dve.wait_ge(su_dve, step)
                    nc.vector.tensor_tensor(mixw[:, :, :], mixw[:, :, :], prod, ALU.add).then_inc(su_dve, 1)
                    step += 1
            dve.wait_ge(su_dve, step)

            dve.wait_ge(pads, 2)

            def split_x(t, s):
                xt = acc[:, bass.ds(t, 1), :].rearrange("p t n -> p (t n)")
                mid = slice(PAD, PAD + HID)
                nc.vector.tensor_copy(x_hi[s][:, mid], xt).then_inc(x_hi_ok, 1)
                dve.wait_ge(x_hi_ok, t + 1)
                nc.vector.tensor_tensor(x_lo[s][:, mid], xt, f32(x_hi[s][:, mid]), ALU.subtract).then_inc(x_split, 1)

            def hT_low(t, s):
                dve.wait_ge(hT_hi_ok, t + 1)
                at = [part[:, :].rearrange("p (k t n) -> p k t n", k=KT, n=P)[:, :, bass.ds(t, 1), :]
                      for part in (hT_hi, hT_lo)]
                nc.vector.tensor_tensor(at[1], q_bank[2 + s][:, :].rearrange("p (k t n) -> p k t n", k=KT, t=1),
                                        f32(at[0]), ALU.subtract).then_inc(hT_ok, 1)

            dve.wait_ge(x_in[0], 16)
            for s in range(2):
                split_x(s, s)
            for q in range(1, 4):
                dve.wait_ge(x_in[q], 16)
            with dve.Fori(1, TILES // 2) as i:
                for s in range(2):
                    dve.wait_ge(conv_done, 2 * i + s - 1)
                    split_x(2 * i + s, s)
                for s in range(2):
                    hT_low(2 * i + s - 2, s)
            for s in range(2):
                hT_low(TILES - 2 + s, s)

            def rope(n):
                used(dve, scores_done, n)
                for j in range(1 + REP):
                    src = k_bank if j == 0 else q_bank[j - 1]
                    dve.wait_ge(proj_done, n * QKV + j + 1)
                    cs = [x.rearrange("p (b q) -> p b q", b=1) for x in (cosT, sinT)]
                    bq = "p (b q) -> p b q"
                    nc.vector.tensor_tensor(rope_c.rearrange(bq, b=BPB), src[:, :].rearrange(bq, b=BPB),
                                            cs[0].to_broadcast([P, BPB, SEQ]), ALU.mult).then_inc(rope_part, 1)
                    for to, fro in ((0, 64), (64, 0)):
                        nc.vector.tensor_tensor(rope_s[to:to + 64, :].rearrange(bq, b=BPB),
                                                src[fro:fro + 64, :].rearrange(bq, b=BPB),
                                                cs[1][fro:fro + 64, :, :].to_broadcast([64, BPB, SEQ]),
                                                ALU.mult).then_inc(rope_part, 1)
                    dve.wait_ge(rope_part, 3 * ((1 + REP) * n + j + 1))
                    dst = roped_k.rearrange(bq, b=BPB) if j == 0 else \
                        roped_q.rearrange("p (b h q) -> p b h q", b=BPB, h=REP)[:, :, j - 1, :]
                    nc.vector.tensor_tensor(dst, rope_c.rearrange(bq, b=BPB), rope_s.rearrange(bq, b=BPB),
                                            ALU.add).then_inc(roped, 1)
                    dve.wait_ge(roped, (1 + REP) * n + j + 1)

            pk = prob.rearrange("p (b k) -> p b k", b=BPB)

            def rows(j):
                return stat[:, j, :].rearrange("p (b o) -> p b o", o=1).to_broadcast([P, BPB, SEQ])

            def softmax_max(n):
                dve.wait_ge(scores_done, n + 1)
                used(dve, pt_done, n)
                nc.vector.tensor_tensor(pk, s_bank[:, :].rearrange("p (b k) -> p b k", b=BPB),
                                        limit.rearrange("p (b k) -> p b k", b=1).to_broadcast([P, BPB, SEQ]),
                                        ALU.min).then_inc(s_read, 1)
                dve.wait_ge(s_read, n + 1)
                nc.vector.tensor_reduce(stat[:, 0, :], pk, AX_X, ALU.max).then_inc(sm_step, 1)
                dve.wait_ge(sm_step, 5 * n + 1)
                nc.vector.tensor_tensor(pk, pk, rows(0), ALU.subtract).then_inc(sm_step, 1)

            def softmax_norm(n):
                dve.wait_ge(exp_done, n + 1)
                nc.vector.tensor_reduce(stat[:, 1, :], pk, AX_X, ALU.add).then_inc(sm_step, 1)
                dve.wait_ge(sm_step, 5 * n + 3)
                nc.vector.reciprocal(stat[:, 2, :], stat[:, 1, :]).then_inc(sm_step, 1)
                dve.wait_ge(sm_step, 5 * n + 4)
                nc.vector.tensor_tensor(pk, pk, rows(2), ALU.mult).then_inc(sm_step, 1)

            def context_lo(n):
                for r in range(BPT):
                    dve.wait_ge(ctx_hi_ok, BPT * n + r + 1)
                    nc.vector.tensor_tensor(context(ctx_lo, r), bank_thq(r), f32(context(ctx_hi, r)),
                                            ALU.subtract).then_inc(ctx_ok, 1)

            def add_out(n, blk, t):
                dve.wait_ge(out_done, TPB * n + t + 1)
                at = acc[:, bass.ds(blk * TPB + t, 1), :].rearrange("p t n -> p (t n)")
                nc.vector.tensor_tensor(at, (k_bank, v_bank)[t % 2][:, :], at, ALU.add).then_inc(out_added, 1)

            def body(n, blk):
                rope(n + 1)
                context_lo(n)
                softmax_max(n + 1)
                add_out(n, blk, 0)
                softmax_norm(n + 1)
                for t in range(1, TPB):
                    add_out(n, blk, t)

            rope(0)
            softmax_max(0)
            softmax_norm(0)
            with dve.Fori(0, KV_HEADS - 1) as g:
                with dve.Fori(0, BLOCKS) as blk:
                    body(g * BLOCKS + blk, blk)
            with dve.Fori(0, BLOCKS - 1) as blk:
                body((KV_HEADS - 1) * BLOCKS + blk, blk)
            context_lo(STEPS - 1)
            dve.wait_ge(lora_in, 16 * LORA_LOADS)
            for k in range(4):
                nc.vector.tensor_tensor(
                    gsel[:, k * 256:(k + 1) * 256].rearrange("p (g r) -> p g r", g=LGROUPS),
                    gateT[:, k * 8:(k + 1) * 8].rearrange("p (g r) -> p g r", r=1).to_broadcast([P, LGROUPS, RANK]),
                    con[:, ID32:ID32 + RANK].rearrange("p (g r) -> p g r", g=1).to_broadcast([P, LGROUPS, RANK]),
                    ALU.mult).then_inc(gsel_ok, 1)
            for t in range(TPB):
                add_out(STEPS - 1, BLOCKS - 1, t)

            catA = [w[:, 0:2048].rearrange("p (k g r) -> p k g r", k=KT, g=LGROUPS) for w in (w_hi, w_lo)]
            for k in range(KT):
                dve.wait_ge(lora_hi, 2 * (k // 2) + 2)
                src = (s_bank, t_bank)[k // 2][:, 256 * (k % 2):256 * (k % 2) + 256]
                nc.vector.tensor_tensor(catA[1][:, k, :, 0:RANK], src.rearrange("p (g r) -> p g r", g=LGROUPS),
                                        f32(catA[0][:, k, :, 0:RANK]), ALU.subtract).then_inc(lora_ok, 1)
            for k in range(KT):
                dve.wait_ge(lora_hi, KT + k + 1)
                nc.vector.tensor_tensor(
                    catA[1][:, k, :, RANK:2 * RANK],
                    sharedA[:, k * RANK:(k + 1) * RANK].rearrange("p (g r) -> p g r", g=1).to_broadcast([P, LGROUPS, RANK]),
                    f32(catA[0][:, k, :, RANK:2 * RANK]), ALU.subtract).then_inc(lora_ok, 1)
            for g in range(LGROUPS):
                dve.wait_ge(lora_hi, 2 * KT + g + 1)
                b = g % 4
                sl = slice(FB + g * 512, FB + (g + 1) * 512)
                nc.vector.tensor_tensor(hT_lo[0:RANK, sl], q_bank[g // 4][b * RANK:(b + 1) * RANK, :],
                                        f32(hT_hi[0:RANK, sl]), ALU.subtract).then_inc(lora_ok, 1)
            for g in range(LGROUPS):
                dve.wait_ge(lora_hi, 2 * KT + LGROUPS + g + 1)
                sl = slice(FB + g * 512, FB + (g + 1) * 512)
                nc.vector.tensor_tensor(hT_lo[RANK:2 * RANK, sl], sharedB, f32(hT_hi[RANK:2 * RANK, sl]),
                                        ALU.subtract).then_inc(lora_ok, 1)
            for g in range(LGROUPS):
                dve.wait_ge(lora_hi, 2 * KT + 2 * LGROUPS + g + 1)
                sl = (slice(2 * RANK, 2 * RANK + 1), slice(FB + g * 512, FB + (g + 1) * 512))
                nc.vector.tensor_tensor(hT_lo[sl], w_scale[2 * RANK:2 * RANK + 1, 0, :], f32(hT_hi[sl]),
                                        ALU.subtract).then_inc(lora_ok, 1)
            with dve.Fori(0, TILES // 2) as i:
                for s in range(2):
                    dve.wait_ge(yT_hi_ok, 2 * i + s + 1)
                    sl = slice(FY + 512 * s, FY + 512 * (s + 1))
                    nc.vector.tensor_tensor(hT_lo[:, sl], q_bank[2 + s][:, :], f32(hT_hi[:, sl]),
                                            ALU.subtract).then_inc(yT_ok, 1)
                for s in range(2):
                    dve.wait_ge(axT_hi_ok, 2 * i + s + 1)
                    sl = slice(FX + P * s, FX + P * (s + 1))
                    nc.vector.tensor_tensor(hT_lo[:, sl], (s_bank, t_bank)[s][:, 128:256], f32(hT_hi[:, sl]),
                                            ALU.subtract).then_inc(axT_ok, 1)
                for s in range(2):
                    dve.wait_ge(ffn_done, 2 * i + s + 1)
                    at = acc[:, bass.ds(2 * i + s, 1), :].rearrange("p t n -> p (t n)")
                    nc.vector.tensor_tensor(at, (k_bank, v_bank)[s][:, :], at, ALU.add).then_inc(result, 1)

        @block.tensor
        def _(pe):
            def three(dst, terms, start=True, stop=True):
                last = None
                for i, ((lh, ll), (rh, rl)) in enumerate(terms):
                    for j, (l, r) in enumerate(((lh, rh), (ll, rh), (lh, rl))):
                        last = nc.tensor.matmul(dst, l, r, start=start and i == 0 and j == 0,
                                                stop=stop and i == len(terms) - 1 and j == 2)
                return last

            pe.wait_ge(con_in, 16)
            pe.wait_ge(set_in, 16 * 13)
            nc.tensor.matmul(s_bank[:, 0:64], su["cwT"], su["condT"], start=True, stop=True).then_inc(su_pe, 1)
            nc.tensor.matmul(t_bank[:, 64:128], su["w0"], su["condT"], start=True, stop=True).then_inc(su_pe, 1)
            pe.wait_ge(cbias_ok, 4)
            pe.wait_ge(su_act, 1)
            nc.tensor.matmul(s_bank[:, 128:192], su["w1"], su["h1"], start=True, stop=True).then_inc(su_pe, 1)
            pe.wait_ge(su_act, 2)
            nc.tensor.matmul(s_bank[0:BATCH, 192:200], su["h2"], su["w2"], start=True, stop=True).then_inc(su_pe, 1)
            pe.wait_ge(su_dve, 6)
            nc.tensor.transpose(s_bank[0:MIX, 256:320], su["att"], ident[0:BATCH, 0:BATCH]).then_inc(su_pe, 1)
            pe.wait_ge(su_dve, 7)
            for k in range(MIX):
                nc.tensor.matmul(t_bank[:, k * 64:(k + 1) * 64], su["sel"][:, k * 128:(k + 1) * 128], su["attT"],
                                 start=True, stop=True)
            nc.tensor.matmul(s_bank[:, 320:384], su["biask"], su["attT"], start=True, stop=True).then_inc(su_pe, 1)

            pe.wait_ge(convw_ok, 3)
            def conv_pair(i):
                for s in range(2):
                    pe.wait_ge(x_split, 2 * i + s + 1)
                    last = three(q_bank[s][:, :],
                                 [((convw_hi[:, k * 128:(k + 1) * 128], convw_lo[:, k * 128:(k + 1) * 128]),
                                   (x_hi[s][:, k:k + HID], x_lo[s][:, k:k + HID])) for k in range(TAPS)])
                    last.then_inc(conv_done, 1)
                for s in range(2):
                    pe.wait_ge(h_ok, 2 * i + s + 1)
                    used(pe, hT_ok, 2 * i)
                    for k in range(KT):
                        last = nc.tensor.transpose(q_bank[2 + s][:, k * P:(k + 1) * P],
                                                   h_tile[s][:, k * P:(k + 1) * P], ident)
                    last.then_inc(ht_done, 1)

            conv_pair(0)
            with pe.Fori(1, TILES // 2) as i:
                conv_pair(i)

            def chunk(c, k):
                sl = slice(c * 512 + k * P, c * 512 + (k + 1) * P)
                return w_hi[:, sl], w_lo[:, sl]

            def project(dst, c, blk):
                return three(dst, [(chunk(c, k), (hT(hT_hi, k, blk * BLOCK, BLOCK), hT(hT_lo, k, blk * BLOCK, BLOCK)))
                                   for k in range(KT)])

            def project_kq(blk, g=None):
                for j in range(1 + REP):
                    if g is not None:
                        pe.wait_ge(w_ready, g * CHUNKS + j + 1)
                    project(k_bank[:, :] if j == 0 else q_bank[j - 1][:, :], C_K + j, blk).then_inc(proj_done, 1)

            def project_v(blk, g=None):
                if g is not None:
                    pe.wait_ge(w_ready, g * CHUNKS + C_V + 1)
                project(v_bank[:, :], C_V, blk).then_inc(proj_done, 1)

            def transpose_probs(n):
                pe.wait_ge(sm_step, 5 * n + 5)
                pe.wait_ge(v_ok, n + 1)
                for t in range(TPB):
                    last = nc.tensor.transpose(t_bank[:, t * P:(t + 1) * P], prob[:, t * P:(t + 1) * P], ident)
                last.then_inc(pt_done, 1)

            def context_of(n):
                pe.wait_ge(probT_ok, n + 1)
                for t in range(TPB):
                    for r in range(BPT):
                        rows = slice(32 * r, 32 * r + 32)
                        last = nc.tensor.matmul(q_bank[r][:, t * P:(t + 1) * P], v_sb[rows, t * P:(t + 1) * P],
                                                probT[rows, t * P:(t + 1) * P], start=True, stop=True)
                last.then_inc(pv_done, 1)

            def scores(n):
                pe.wait_ge(vT_ok, n + 1)
                for t in range(TPB):
                    last = nc.tensor.transpose(t_bank[:, t * P:(t + 1) * P], vT[:, t * P:(t + 1) * P], ident)
                last.then_inc(vt_done, 1)
                pe.wait_ge(roped, (1 + REP) * (n + 1))
                used(pe, s_read, n)
                for b in range(BPB):
                    last = nc.tensor.matmul(s_bank[:, b * SEQ:(b + 1) * SEQ], roped_q[:, b * P:(b + 1) * P],
                                            roped_k[:, b * SEQ:(b + 1) * SEQ], start=True, stop=True)
                last.then_inc(scores_done, 1)

            def project_out(n, g=None):
                if g is not None:
                    pe.wait_ge(w_ready, (g + 1) * CHUNKS)
                pe.wait_ge(ctx_ok, BPT * (n + 1))
                for t in range(TPB):
                    if t >= 2:
                        pe.wait_ge(out_added, TPB * n + t - 1)
                    last = three((k_bank, v_bank)[t % 2][:, :],
                                 [((ctx_hi[:, h * BLOCK + t * P:h * BLOCK + (t + 1) * P],
                                    ctx_lo[:, h * BLOCK + t * P:h * BLOCK + (t + 1) * P]),
                                   (w_hi[:, (C_O + h) * 512:(C_O + h + 1) * 512],
                                    w_lo[:, (C_O + h) * 512:(C_O + h + 1) * 512])) for h in range(REP)])
                    last.then_inc(out_done, 1)

            def body(n, blk, g=None, first=None):
                used(pe, ctx_ok, BPT * n)
                used(pe, out_added, TPB * n)
                project_kq(blk, g)
                transpose_probs(n)
                project_v(blk, g)
                pe.wait_ge(rope_part, 3 * (1 + REP) * (n + 2))
                context_of(n)
                scores(n + 1)
                project_out(n, first)

            pe.wait_ge(hT_ok, TILES)
            pe.wait_ge(su_dve, 7 + 2 * BPT)
            project_kq(0, 0)
            project_v(0, 0)
            scores(0)
            body(0, 1, first=0)
            with pe.Fori(1, BLOCKS - 1) as blk:
                body(blk, blk + 1)
            body(BLOCKS - 1, 0, g=1)
            with pe.Fori(1, KV_HEADS - 1) as g:
                body(g * BLOCKS, 1, first=g)
                with pe.Fori(1, BLOCKS - 1) as blk:
                    body(g * BLOCKS + blk, blk + 1)
                body(g * BLOCKS + BLOCKS - 1, 0, g=g + 1)
            base = (KV_HEADS - 1) * BLOCKS
            body(base, 1, first=KV_HEADS - 1)
            with pe.Fori(1, BLOCKS - 1) as blk:
                body(base + blk, blk + 1)
            transpose_probs(STEPS - 1)
            context_of(STEPS - 1)

            pe.wait_ge(gsel_ok, 4)
            for k in range(KT):
                dst = (s_bank, t_bank)[k // 2][:, 256 * (k % 2):256 * (k % 2) + 256]
                for part in range(4):
                    last = nc.tensor.matmul(dst, loraA[:, part * 512 + k * P:part * 512 + (k + 1) * P],
                                            gsel[:, part * 256:(part + 1) * 256], start=part == 0, stop=part == 3)
            last.then_inc(lora_pe, 1)
            project_out(STEPS - 1)
            for j in range(2):
                for part in range(4):
                    last = nc.tensor.matmul(q_bank[j][:, :],
                                            gsel[:, part * 256 + j * P:part * 256 + (j + 1) * P],
                                            loraB[:, part * 512:(part + 1) * 512], start=part == 0, stop=part == 3)
                last.then_inc(lora_pe, 1)

            pe.wait_ge(lora_ok, 32)
            pe.wait_ge(rest_ok, 6)
            pe.wait_ge(kern_ok, 1)
            pe.wait_ge(out_added, TPB * STEPS)

            def feed_forward_pair(i):
                for s in range(2):
                    pe.wait_ge(bd_ok, 2 * i + s + 1)
                    nc.tensor.matmul(q_bank[s][:, :], mixbd[s],
                                     acc[:, bass.ds(2 * i + s, 1), :].rearrange("p t n -> p (t n)"),
                                     start=True, stop=True).then_inc(y_done, 1)
                for s in range(2):
                    pe.wait_ge(y_ok, 2 * i + s + 1)
                    for k in range(KT):
                        last = nc.tensor.transpose(q_bank[2 + s][:, k * P:(k + 1) * P],
                                                   y_sb[s][:, k * P:(k + 1) * P], ident)
                    last.then_inc(yt_done, 1)

                def yT(s, k):
                    sl = slice(FY + 512 * s + k * P, FY + 512 * s + (k + 1) * P)
                    return hT_hi[:, sl], hT_lo[:, sl]

                for s in range(2):
                    pe.wait_ge(yT_ok, 2 * i + s + 1)
                    if s == 0:
                        used(pe, axT_ok, 2 * i)
                    three((s_bank, t_bank)[s][:, 0:2 * RANK],
                          [(yT(s, k), tuple(w[:, bass.ds(i * 64 + k * 512, 64)] for w in (w_hi, w_lo)))
                           for k in range(KT)]).then_inc(ax_done, 1)
                used(pe, result, 2 * i)
                for s in range(2):
                    three((k_bank, v_bank)[s][:, :],
                          [(yT(s, k), (hT_hi[:, FK + k * 512:FK + (k + 1) * 512],
                                       hT_lo[:, FK + k * 512:FK + (k + 1) * 512])) for k in range(KT)], stop=False)
                    pe.wait_ge(ax_ok, 2 * i + s + 1)
                    nc.tensor.transpose((s_bank, t_bank)[s][:, 128:256], ax_sb[s], ident).then_inc(axt_done, 1)
                for s in range(2):
                    pe.wait_ge(axT_ok, 2 * i + s + 1)
                    three((k_bank, v_bank)[s][:, :],
                          [((hT_hi[:, FX + P * s:FX + P * (s + 1)], hT_lo[:, FX + P * s:FX + P * (s + 1)]),
                            (hT_hi[:, bass.ds(FB + i * 512, 512)], hT_lo[:, bass.ds(FB + i * 512, 512)]))],
                          start=False).then_inc(ffn_done, 1)

            feed_forward_pair(0)
            with pe.Fori(1, TILES // 2) as i:
                feed_forward_pair(i)


def constants():
    import numpy as np
    con = np.zeros((P, CON_N), np.float32)
    p = np.arange(P)
    inv = (1.0 / np.float32(10000.0) ** (np.arange(0, HEAD, 2, dtype=np.float32) / np.float32(HEAD))).astype(np.float32)
    freq = np.arange(SEQ, dtype=np.float32)[:, None] * inv
    con[:, COS:COS + SEQ] = np.concatenate([np.cos(freq), np.cos(freq)], 1).T
    con[:, SIN:SIN + SEQ] = np.concatenate([np.sin(freq), -np.sin(freq)], 1).T
    big = np.finfo(np.float32)
    con[:, LIM:LIM + SEQ] = np.where(np.arange(SEQ)[None] <= (p % SEQ)[:, None], big.max, big.min)
    con[:, IDN:IDN + P] = np.eye(P, dtype=np.float32)
    con[:, BD8:BD8 + 16] = (p[:, None] // 8 == np.arange(16)[None])
    con[:, BD32:BD32 + BPT] = (p[:, None] // 32 == np.arange(BPT)[None])
    con[:, ID32:ID32 + 32] = (p[:, None] % 32 == np.arange(32)[None])
    sel = np.zeros((MIX, MIX, P), np.float32)
    for k in range(MIX):
        sel[k, k] = 1.0
    return con, sel.reshape(MIX, MIX * P)


def kernel(**inputs):
    import numpy as np
    import concourse.bacc as bacc
    from concourse import mybir as mb
    from concourse.bass_utils import run_bass_kernel_spmd

    i = {k: np.asarray(v) for k, v in inputs.items()}
    c = np.ascontiguousarray

    def proj(w):
        return w.reshape(KT, P, -1, P).transpose(2, 1, 0, 3).reshape(-1, P, 512)

    def srow(w):
        return w.reshape(KT, -1, P).transpose(1, 0, 2).reshape(-1, 512)

    def group(k, q, v, o):
        return c(np.concatenate([k[:, None], q.reshape(KV_HEADS, REP, *q.shape[1:]), v[:, None],
                                 o.reshape(KV_HEADS, REP, *o.shape[1:])], axis=1))

    con, sel = constants()
    arrays = {
        "con": con, "sel": sel,
        "x": c(i["x"].reshape(TILES, P, HID)),
        "condT": c(i["cond_128"].T),
        "fb": c(np.tile(i["fside_S_0"], BPT).reshape(P, 1)),
        "t72": c(np.tile(i["L0_cond_weight"].reshape(4, 8, 8, TAPS).transpose(0, 2, 3, 1).reshape(32, TAPS * 8), (BPT, 1))),
        "cwT": c(np.tile(i["L0_cond_c_weight"].T, (1, BPT))),
        "w0": c(i["L0_cond2_W0"]), "w1": c(i["L0_cond2_W1"]), "w2": c(i["L0_cond2_W2"]),
        "b0": c(i["L0_cond2_b0"].reshape(P, 1)), "b1": c(i["L0_cond2_b1"].reshape(P, 1)),
        "b2": c(i["L0_cond2_b2"].reshape(1, MIX)),
        "biask": c(np.tile(i["L0_cond2_bias_k"], (1, BPT))),
        "mixk": c(np.tile(i["L0_cond2_weight"][..., 0].transpose(2, 0, 1).reshape(32, MIX * 32), (BPT, 1))),
        "qw": group(proj(i["L0_attn_qw_k"]), proj(i["L0_attn_qw_q"]), proj(i["L0_attn_qw_v"]),
                    i["L0_attn_qw_o"].reshape(-1, P, 512)),
        "scales": group(srow(i["L0_attn_scales_k"]), srow(i["L0_attn_scales_q"]), srow(i["L0_attn_scales_v"]),
                        i["L0_attn_scales_o"].reshape(-1, 512)),
        "kern": c(i["L0_ffn_kernel"].reshape(KT, P, 512).transpose(1, 0, 2)),
        "fbias": c(i["L0_ffn_bias"].reshape(1, HID)),
        "loraA": c(i["L0_ffn_lora_A"].reshape(4, P, 512).transpose(1, 0, 2)),
        "loraB": c(i["L0_ffn_lora_B"].transpose(0, 2, 1).reshape(4, P, 512).transpose(1, 0, 2)),
        "gateT": c(i["L0_ffn_gate"].T.reshape(4, 4, LGROUPS).transpose(1, 0, 2).reshape(4, 32)),
        "sharedA": c(i["L0_ffn_lora_A_shared"].T.reshape(KT, P, RANK).transpose(1, 0, 2).reshape(P, KT * RANK)),
        "sharedB": c(i["L0_ffn_lora_B_shared"].T),
    }
    nc = bacc.Bacc("TRN2", target_bir_lowering=False, num_devices=1)
    aps = {k: nc.dram_tensor(f"in_{k}", v.shape, mb.dt.from_np(v.dtype), kind="ExternalInput").ap()
           for k, v in arrays.items()}
    out = nc.dram_tensor("out_x", (TILES // 2, 2, P, HID), mb.dt.from_np(np.dtype("float32")), kind="ExternalOutput").ap()
    build(nc, aps, out.rearrange("i t p n -> i p t n"))
    r = run_bass_kernel_spmd(nc, [{f"in_{k}": v for k, v in arrays.items()}], core_ids=[0])
    return r.results[0]["out_x"].reshape(BATCH, SEQ, HID)
```

```python
from contextlib import ExitStack

import concourse.bass as bass
from concourse import mybir

F32 = mybir.dt.float32
F32R = mybir.dt.float32r
I32 = mybir.dt.int32
ALU = mybir.AluOpType
ACT = mybir.ActivationFunctionType
AX_X = mybir.AxisListType.X

P = 128
BATCH, SEQ, HID = 64, 32, 512
TOKENS = BATCH * SEQ
TILES = TOKENS // P
BPT = P // SEQ
KT = HID // P
HEAD = 128
KV_HEADS = 8
REP = 4
BLOCK = 512
TPB = BLOCK // P
BPB = BLOCK // SEQ
BLOCKS = TOKENS // BLOCK
STEPS = KV_HEADS * BLOCKS
TAPS, PAD = 9, 4
XW = HID + 2 * PAD
MIX = 8
NLORA, RANK = 16, 32
LGROUPS = 8
ZERO_POINT = 8.0

C_K, C_Q, C_V = 0, 1, 5
CHUNKS = 6
PARTS = REP * KT

COS, SIN, LIM, IDN, BD8, BD32, ID32, CON_N = 0, 32, 64, 96, 224, 240, 244, 276


def build(nc, a, out):
    ctx = ExitStack()
    with ctx:
        def sb(name, shape, dt=F32):
            return ctx.enter_context(nc.sbuf_tensor(name, shape, dt))

        def sem(name):
            return ctx.enter_context(nc.semaphore(name))

        bank = [ctx.enter_context(nc.psum_tensor(f"bank{i}", [P, 512], F32)) for i in range(8)]
        q_bank, k_bank, v_bank, s_bank, t_bank = bank[0:4], bank[4], bank[5], bank[6], bank[7]

        acc = sb("acc", [P, TILES * HID])
        hT_hi = sb("hT_hi", [P, KT * TOKENS], F32R)
        hT_lo = sb("hT_lo", [P, KT * TOKENS], F32R)
        w_hi = sb("w_hi", [P, CHUNKS * 512], F32R)
        w_lo = sb("w_lo", [P, CHUNKS * 512], F32R)
        w32 = sb("w32", [P, CHUNKS * 512])
        w_scale = sb("w_scale", [P, 2, 512])
        wo_land = sb("wo_land", [P, REP * HID])
        wo = sb("wo", [P, REP * HID], F32R)
        wo_scale = sb("wo_scale", [P, KV_HEADS * PARTS])
        ctx_hi = sb("ctx_hi", [P, REP * BLOCK], F32R)
        ctx_lo = sb("ctx_lo", [P, REP * BLOCK], F32R)
        v_sb = [sb(f"v_sb{i}", [P, BLOCK])[:, :] for i in range(2)]
        work = sb("work", [P, 6656])
        con = sb("con", [P, CON_N])
        mixw = sb("mixw", [P, TILES, SEQ])
        cbias = sb("cbias", [P, TILES])
        mbias = sb("mbias", [P, TILES])
        stat = sb("stat", [P, 3, BPB])

        roped_q = work[:, 0:2048]
        rope_c = [work[:, 2048 + 1024 * j:2560 + 1024 * j] for j in range(2)]
        rope_s = [work[:, 2560 + 1024 * j:3072 + 1024 * j] for j in range(2)]
        roped_k = work[:, 4096:4608]
        vT = work[:, 4608:5120]
        scoreT = work[:, 5120:5632]
        prob = work[:, 5632:6144]
        probT = work[:, 6144:6656]

        cosT, sinT, limit = con[:, COS:COS + 32], con[:, SIN:SIN + 32], con[:, LIM:LIM + 32]
        ident = con[:, IDN:IDN + 128]

        h_tile = [work[:, 512 * s:512 * s + 512] for s in range(2)]
        o = 1024
        su = {}
        for name, rows, n in (("t72", P, TAPS * 8), ("condT", P, BATCH), ("w0", P, 128), ("w1", P, 128),
                              ("w2", P, MIX), ("cwT", P, 128), ("b0", P, 1), ("b1", P, 1), ("fb", P, 1),
                              ("b2", BATCH, MIX), ("biask", MIX, 128), ("sel", MIX, MIX * 128),
                              ("mixk", P, MIX * 32), ("h1", P, BATCH), ("h2", P, BATCH), ("att", BATCH, MIX),
                              ("attT", MIX, BATCH), ("attR", P, MIX * TILES), ("prod", P, 512),
                              ("convw", P, TAPS * 128)):
            su[name] = work[0:rows, o:o + n]
            o += n
        assert o <= 6656
        convw, convw_hi = su["convw"], wo[:, 0:TAPS * 128]
        taps_in_wo = (REP * HID - TAPS * 128) // 128
        convw_lo = [(0, wo[:, TAPS * 128:]), (taps_in_wo, ctx_lo[:, 2 * XW:2 * XW + (TAPS - taps_in_wo) * 128])]
        x_hi = [ctx_hi[:, s * XW:(s + 1) * XW] for s in range(2)]
        x_lo = [ctx_lo[:, s * XW:(s + 1) * XW] for s in range(2)]

        FK, FB, FY = 0, 2048, 6144
        loraA = wo_land[:, :]
        loraB = w32[:, 0:2048]
        gateT = w32[:, 2048:2080]
        sharedA = w32[:, 2080:2208]
        sharedB = w32[32:64, 2208:2720]
        bias_row = w32[64:65, 2208:2720]
        gsel = w_scale[:, :, :].rearrange("p a b -> p (a b)")
        kern = work[:, 0:2048]
        at_sb = [work[:, 2048 + 512 * s:2560 + 512 * s] for s in range(2)]
        y_sb = [work[:, 3072 + 512 * s:3584 + 512 * s] for s in range(2)]
        ax_sb = [work[:, 4096 + 128 * s:4224 + 128 * s] for s in range(2)]
        x_sb = work[:, 4608:5632]
        mixbd = [work[:, 5632 + 128 * s:5760 + 128 * s] for s in range(2)]
        axT = [[part[:, P * s:P * (s + 1)] for s in range(2)] for part in (ctx_hi, ctx_lo)]
        yT_all = [[part[:, FY + 512 * s:FY + 512 * (s + 1)] for s in range(2)] for part in (hT_hi, hT_lo)]

        con_in, set_in = sem("con_in"), sem("set_in")
        x_in = [sem(f"x_in{i}") for i in range(4)]
        su_pe, su_act, su_dve = sem("su_pe"), sem("su_act"), sem("su_dve")
        cbias_ok, convw_ok, pads = sem("cbias_ok"), sem("convw_ok"), sem("pads")
        x_hi_ok, x_split = sem("x_hi_ok"), sem("x_split")
        conv_done, h_ok, ht_done, hT_hi_ok, hT_ok = (sem(n) for n in
                                                     ("conv_done", "h_ok", "ht_done", "hT_hi_ok", "hT_ok"))
        w_in = [sem(f"w_in{c}") for c in range(CHUNKS)]
        scale_in = [sem(f"scale_in{s}") for s in range(2)]
        w_zeroed, w_scaled, w_hi_ok, w_ready = (sem(n) for n in ("w_zeroed", "w_scaled", "w_hi_ok", "w_ready"))
        wo_in, wo_ready, wo_scale_in = sem("wo_in"), sem("wo_ready"), sem("wo_scale_in")
        k_done, q_done, v_done = sem("k_done"), sem("q_done"), sem("v_done")
        k_swapped, k_cos, k_sin, k_roped = sem("k_swapped"), sem("k_cos"), sem("k_sin"), sem("k_roped")
        q_swapped, q_cos, q_sin, q_roped = sem("q_swapped"), sem("q_cos"), sem("q_sin"), sem("q_roped")
        vT_ok, vt_done, v_ok = sem("vT_ok"), sem("vt_done"), sem("v_ok")
        scores_done, st_ok, turned, s_read = sem("scores_done"), sem("st_ok"), sem("turned"), sem("s_read")
        sm_step, exp_done = sem("sm_step"), sem("exp_done")
        pt_done, probT_ok, pv_done = sem("pt_done"), sem("probT_ok"), sem("pv_done")
        ctx_hi_ok, ctx_ok = sem("ctx_hi_ok"), sem("ctx_ok")
        out_done, out_added, acc_zero = sem("out_done"), sem("out_added"), sem("acc_zero")
        lora_in, kern_in, gsel_ok = sem("lora_in"), sem("kern_in"), sem("gsel_ok")
        lora_pe, lora_hi, lora_ok = sem("lora_pe"), sem("lora_hi"), sem("lora_ok")
        kern_hi, kern_ok, rest_ok = sem("kern_hi"), sem("kern_ok"), sem("rest_ok")
        at_ok, tx_done, xs_in, x1_ok = sem("at_ok"), sem("tx_done"), sem("xs_in"), sem("x1_ok")
        bd_ok, y_done, y_ok, yt_done, yT_hi_ok, yT_ok = (sem(n) for n in
                                                         ("bd_ok", "y_done", "y_ok", "yt_done", "yT_hi_ok", "yT_ok"))
        ax_done, ax_ok, axt_done, axT_hi_ok, axT_ok = (sem(n) for n in
                                                       ("ax_done", "ax_ok", "axt_done", "axT_hi_ok", "axT_ok"))
        kern_used, ffn_done, result, stored = sem("kern_used"), sem("ffn_done"), sem("result"), sem("stored")

        CONV_LOADS, MLP_LOADS = 4, 9
        LORA_LOADS = 5 + P // RANK

        block = ctx.enter_context(nc.Block())

        def f32(ap):
            return ap.bitcast(F32)

        def hT(part, kt, tok0, n):
            return part[:, bass.ds(tok0 + kt * TOKENS, n)]

        def tile_of(t):
            return acc[:, bass.ds(t * HID, HID)]

        def turned_tile(t):
            return acc[:, :].rearrange("p (k t n) -> p k t n", k=KT, n=P)[:, :, bass.ds(t, 1), :]

        def ktn(ap):
            return ap.rearrange("p (k t n) -> p k t n", k=KT, t=1)

        def used(eng, signal, count):
            if not isinstance(count, int) or count > 0:
                eng.wait_ge(signal, count)

        def context(part, r):
            return part[:, :].rearrange("p (h t b q) -> p t h b q", h=REP, t=TPB, b=BPT)[:, :, :, r, :]

        def bank_thq(r):
            return q_bank[r][:, :].rearrange("p (t h q) -> p t h q", t=TPB, h=REP)

        @block.sync
        def _(sp):
            sp.dma_start(con[:, :], a["con"]).then_inc(con_in, 16)
            for name in ("t72", "cwT", "condT", "fb"):
                sp.dma_start(su[name], a[name]).then_inc(con_in, 16)
            for name in ("w0", "w1", "w2", "b0", "b1", "biask", "sel", "mixk"):
                sp.dma_start(su[name], a[name]).then_inc(set_in, 16)
            sp.dma_start(su["b2"], a["b2"].to_broadcast([BATCH, MIX])).then_inc(set_in, 16)

            def load(g, c):
                sp.dma_start(w32[:, c * 512:(c + 1) * 512].bitcast(I32),
                             a["qw"][g, c, :, :]).then_inc(w_in[c], 16)

            def load_scale(g, c):
                sp.dma_start(w_scale[:, c % 2, :],
                             a["scales"][g, c:c + 1, :].to_broadcast([P, 512])).then_inc(scale_in[c % 2], 16)

            def load_wo(g):
                sp.dma_start(wo_land[:, :].bitcast(I32), a["wo"][g, :, :]).then_inc(wo_in, 16)

            sp.dma_start(wo_scale[:, :], a["wo_scale"]).then_inc(wo_scale_in, 16)
            sp.wait_ge(x_in[3], 16)
            for c in range(CHUNKS):
                load(0, c)
                if c >= 2:
                    sp.wait_ge(w_scaled, c - 1)
                load_scale(0, c)
            load_wo(0)
            with sp.Fori(1, KV_HEADS) as g:
                for c in range(CHUNKS):
                    sp.wait_ge(w_ready, (g - 1) * CHUNKS + c + 1)
                    load(g, c)
                for c in range(CHUNKS):
                    sp.wait_ge(w_scaled, g * CHUNKS + c - 1)
                    load_scale(g, c)
                    if c == 1:
                        sp.wait_ge(wo_ready, g)
                        load_wo(g)
            sp.wait_ge(w_ready, KV_HEADS * CHUNKS)
            sp.dma_start(loraB.rearrange("p (t n) -> p t n", t=4), a["loraB"]).then_inc(lora_in, 16)
            for q in range(P // RANK):
                sp.dma_start(gateT[q * RANK:(q + 1) * RANK, :],
                             a["gateT"][q:q + 1, :].to_broadcast([RANK, 32])).then_inc(lora_in, 16)
            sp.dma_start(sharedA, a["sharedA"]).then_inc(lora_in, 16)
            sp.dma_start(sharedB, a["sharedB"]).then_inc(lora_in, 16)
            sp.dma_start(bias_row, a["fbias"]).then_inc(lora_in, 16)
            sp.wait_ge(wo_ready, KV_HEADS)
            sp.dma_start(loraA.rearrange("p (t n) -> p t n", t=4), a["loraA"]).then_inc(lora_in, 16)
            sp.wait_ge(scores_done, STEPS)
            sp.dma_start(kern.rearrange("p (t n) -> p t n", t=KT), a["kern"]).then_inc(kern_in, 16)

            def load_x(i):
                sp.dma_start(x_sb.rearrange("p (t n) -> p t n", t=2),
                             a["x"][bass.ds(2 * i, 2), :, :].rearrange("t p n -> p t n")).then_inc(xs_in, 16)

            def store(i):
                sp.wait_ge(result, 2 * i + 2)
                for s in range(2):
                    sp.dma_start(out[bass.ds(2 * i + s, 1), :, :].rearrange("t p (k n) -> p k t n", k=KT),
                                 turned_tile(2 * i + s)).then_inc(stored, 16)

            sp.wait_ge(pv_done, BPT * STEPS)
            load_x(0)
            sp.wait_ge(x1_ok, 2)
            load_x(1)
            with sp.Fori(0, TILES // 2 - 2) as i:
                sp.wait_ge(x1_ok, 2 * i + 4)
                load_x(i + 2)
                store(i)
            for i in range(TILES // 2 - 2, TILES // 2):
                store(i)
            sp.wait_ge(stored, 16 * TILES)

        @block.gpsimd
        def _(pool):
            def scale(g, c):
                w = w32[:, c * 512:(c + 1) * 512]
                pool.wait_ge(w_zeroed, g * CHUNKS + c + 1)
                pool.wait_ge(scale_in[c % 2], 16 * (g * (CHUNKS // 2) + c // 2 + 1))
                nc.gpsimd.tensor_tensor(w, w, w_scale[:, c % 2, :], ALU.mult).then_inc(w_scaled, 1)

            def low(g, c):
                sl = slice(c * 512, (c + 1) * 512)
                pool.wait_ge(w_hi_ok, g * CHUNKS + c + 1)
                nc.gpsimd.tensor_tensor(w_lo[:, sl], w32[:, sl], f32(w_hi[:, sl]), ALU.subtract).then_inc(w_ready, 1)

            sine = sinT.rearrange("p (b q) -> p b q", b=1).to_broadcast([P, BPB, SEQ])

            def add_q(n, h):
                i = REP * n + h
                s = rope_s[h % 2].rearrange("p (b q) -> p b q", b=BPB)
                pool.wait_ge(q_swapped, 2 * i + 2)
                nc.gpsimd.tensor_tensor(s, s, sine, ALU.mult).then_inc(q_sin, 1)
                pool.wait_ge(q_sin, i + 1)
                pool.wait_ge(q_cos, i + 1)
                used(pool, scores_done, n)
                nc.gpsimd.tensor_tensor(roped_q.rearrange("p (b h q) -> p b h q", b=BPB, h=REP)[:, :, h, :],
                                        rope_c[h % 2].rearrange("p (b q) -> p b q", b=BPB),
                                        s, ALU.add).then_inc(q_roped, 1)

            def add_k(n):
                s = rope_s[0].rearrange("p (b q) -> p b q", b=BPB)
                pool.wait_ge(k_swapped, 2 * n + 2)
                nc.gpsimd.tensor_tensor(s, s, sine, ALU.mult).then_inc(k_sin, 1)
                pool.wait_ge(k_sin, n + 1)
                pool.wait_ge(k_cos, n + 1)
                used(pool, scores_done, n)
                nc.gpsimd.tensor_tensor(roped_k, rope_c[0], rope_s[0], ALU.add).then_inc(k_roped, 1)

            def body(n, after_q=None, before_k=None, after_k=None, last=False):
                for h in range(REP):
                    add_q(n + 1, h)
                    if after_q and h != REP - 2:
                        for j in ((h,) if h < REP - 2 else (REP - 2, REP - 1)):
                            after_q(j)
                if before_k:
                    before_k()
                if not last:
                    add_k(n + 2)
                if after_k:
                    after_k()

            def group(g):
                def last_scales():
                    for c in range(REP, CHUNKS):
                        scale(g + 1, c)

                body(g * BLOCKS)
                body(g * BLOCKS + 1, after_q=lambda h: scale(g + 1, h), before_k=last_scales,
                     after_k=lambda: low(g + 1, C_K))
                body(g * BLOCKS + 2, after_q=lambda h: low(g + 1, C_Q + h), after_k=lambda: low(g + 1, C_V))
                body(g * BLOCKS + 3)

            for c in range(CHUNKS):
                scale(0, c)
            for c in range(CHUNKS):
                low(0, c)
            add_k(0)
            for h in range(REP):
                add_q(0, h)
            add_k(1)
            pool.wait_ge(x_split, TILES)
            nc.gpsimd.memset(acc[:, :], 0.0).then_inc(acc_zero, 1)
            group(0)
            with pool.Fori(1, KV_HEADS - 1) as g:
                group(g)
            base = (KV_HEADS - 1) * BLOCKS
            body(base)
            body(base + 1)
            body(base + 2, last=True)

            rest = slice(2 * RANK, P)
            pool.wait_ge(v_done, STEPS)
            pool.wait_ge(q_roped, REP * STEPS)
            nc.gpsimd.memset(f32(hT_hi[rest, FB:FB + 4096]), 0.0).then_inc(rest_ok, 1)
            pool.wait_ge(rest_ok, 1)
            nc.gpsimd.memset(f32(hT_lo[rest, FB:FB + 4096]), 0.0).then_inc(rest_ok, 1)
            pool.wait_ge(rest_ok, 2)
            pool.wait_ge(scores_done, STEPS)
            for s in range(2):
                nc.gpsimd.memset(ax_sb[s][:, 2 * RANK:P], 0.0).then_inc(rest_ok, 1)
            pool.wait_ge(rest_ok, 4)
            for s in range(2):
                nc.gpsimd.memset(ax_sb[s][:, 2 * RANK:2 * RANK + 1], 1.0).then_inc(rest_ok, 1)
            pool.wait_ge(kern_in, 16)
            nc.gpsimd.tensor_copy(hT_hi[:, FK:FK + 2048], kern).then_inc(kern_hi, 1)
            pool.wait_ge(kern_hi, 1)
            nc.gpsimd.tensor_tensor(hT_lo[:, FK:FK + 2048], kern, f32(hT_hi[:, FK:FK + 2048]),
                                    ALU.subtract).then_inc(kern_ok, 1)

            def block_diagonal(t, s):
                nc.gpsimd.tensor_tensor(
                    mixbd[s].rearrange("p (b o) -> p b o", b=BPT),
                    mixw[:, bass.ds(t, 1), :].to_broadcast([P, BPT, SEQ]),
                    con[:, BD32:BD32 + BPT].rearrange("p (b o) -> p b o", o=1).to_broadcast([P, BPT, SEQ]),
                    ALU.mult).then_inc(bd_ok, 1)

            pool.wait_ge(pt_done, STEPS)
            for s in range(2):
                block_diagonal(s, s)
            with pool.Fori(1, TILES // 2) as i:
                for s in range(2):
                    pool.wait_ge(y_done, 2 * i + s - 1)
                    block_diagonal(2 * i + s, s)

        @block.scalar
        def _(act):
            for q in range(4):
                if q == 1:
                    act.wait_ge(set_in, 16 * MLP_LOADS)
                act.dma_start(acc[:, 4 * q * HID:4 * (q + 1) * HID].rearrange("p (t n) -> p t n", t=4),
                              a["x"][4 * q:4 * q + 4, :, :].rearrange("t p n -> p t n")).then_inc(x_in[q], 16)
            act.wait_ge(su_pe, 2)
            nc.scalar.activation(su["h1"], t_bank[:, 64:128], ACT.Gelu, bias=su["b0"]).then_inc(su_act, 1)
            act.wait_ge(su_pe, 3)
            nc.scalar.activation(su["h2"], s_bank[:, 128:192], ACT.Gelu, bias=su["b1"]).then_inc(su_act, 1)
            act.wait_ge(su_dve, 3)
            nc.scalar.activation(su["att"], su["att"], ACT.Exp).then_inc(su_act, 1)

            def zero_point(g, c):
                w = w32[:, c * 512:(c + 1) * 512]
                act.wait_ge(w_in[c], 16 * (g + 1))
                nc.scalar.activation(w, w.bitcast(I32), ACT.Copy, bias=-ZERO_POINT).then_inc(w_zeroed, 1)

            def high(g, c):
                sl = slice(c * 512, (c + 1) * 512)
                act.wait_ge(w_scaled, g * CHUNKS + c + 1)
                nc.scalar.activation(w_hi[:, sl], w32[:, sl], ACT.Identity).then_inc(w_hi_ok, 1)

            def take_wo(g):
                act.wait_ge(wo_in, 16 * (g + 1))
                used(act, out_done, PARTS * BLOCKS * g)
                nc.scalar.activation(wo[:, :], wo_land[:, :].bitcast(I32), ACT.Copy, bias=-ZERO_POINT).then_inc(wo_ready, 1)

            def conv_pair(i):
                for s in range(2):
                    act.wait_ge(conv_done, 2 * i + s + 1)
                    act.wait_ge(cbias_ok, 4)
                    used(act, ht_done, 2 * i)
                    nc.scalar.activation(h_tile[s], q_bank[s][:, :], ACT.Identity,
                                         bias=cbias[:, bass.ds(2 * i + s, 1)]).then_inc(h_ok, 1)
                for s in range(2):
                    act.wait_ge(ht_done, 2 * i + s + 1)
                    nc.scalar.activation(
                        hT_hi[:, :].rearrange("p (k t n) -> p k t n", k=KT, n=P)[:, :, bass.ds(2 * i + s, 1), :],
                        ktn(q_bank[2 + s][:, :]), ACT.Identity).then_inc(hT_hi_ok, 1)

            conv_pair(0)
            conv_pair(1)
            conv_pair(2)
            for c in range(CHUNKS):
                zero_point(0, c)
            conv_pair(3)
            conv_pair(4)
            for c in range(CHUNKS):
                high(0, c)
            with act.Fori(5, TILES // 2) as i:
                conv_pair(i)

            def swap(dst, src, signal):
                for to, fro in ((0, 64), (64, 0)):
                    nc.scalar.activation(dst[to:to + 64, :], src[fro:fro + 64, :], ACT.Identity).then_inc(signal, 1)

            def swap_q(n, h):
                act.wait_ge(q_done, REP * n + h + 1)
                if h == 0:
                    act.wait_ge(k_roped, n + 1)
                else:
                    used(act, q_roped, REP * n + h - 1)
                swap(rope_s[h % 2], q_bank[h], q_swapped)

            def swap_k(n):
                act.wait_ge(k_done, n + 1)
                used(act, q_roped, REP * n - 1)
                swap(rope_s[0], k_bank, k_swapped)

            def copy_vT(n):
                act.wait_ge(v_done, n + 1)
                used(act, vt_done, n)
                nc.scalar.activation(vT, v_bank[:, :], ACT.Identity).then_inc(vT_ok, 1)

            def copy_v(n, s):
                act.wait_ge(vt_done, n + 1)
                used(act, pv_done, BPT * (n - 1))
                nc.scalar.activation(v_sb[s], t_bank[:, :], ACT.Identity).then_inc(v_ok, 1)

            def copy_scores(n):
                act.wait_ge(scores_done, n + 1)
                used(act, turned, n)
                nc.scalar.activation(scoreT, s_bank[:, :], ACT.Identity).then_inc(st_ok, 1)

            def exps(n):
                act.wait_ge(sm_step, 5 * n + 2)
                nc.scalar.activation(prob, prob, ACT.Exp, scale=HEAD ** -0.5).then_inc(exp_done, 1)

            def copy_probT(n):
                act.wait_ge(pt_done, n + 1)
                nc.scalar.activation(probT, t_bank[:, :], ACT.Identity).then_inc(probT_ok, 1)

            def context_hi(n):
                used(act, out_done, PARTS * n)
                for r in range(BPT):
                    act.wait_ge(pv_done, BPT * n + r + 1)
                    nc.scalar.activation(context(ctx_hi, r), bank_thq(r), ACT.Identity).then_inc(ctx_hi_ok, 1)

            def body(n, b, after_q=None, after_k=None, last=False):
                for h in range(REP):
                    swap_q(n + 1, h)
                    if h == REP - 1:
                        copy_probT(n)
                    if after_q:
                        after_q(h)
                copy_vT(n + 1)
                copy_scores(n + 1)
                copy_v(n + 1, (b + 1) % 2)
                context_hi(n)
                exps(n + 1)
                if not last:
                    swap_k(n + 2)
                if after_k:
                    after_k()

            def group(g, first=False):
                def zero_points(h):
                    for c in ((0, 1), (2, 3), (4,), (5,))[h]:
                        zero_point(g + 1, c)

                def high_keys():
                    act.wait_ge(k_done, (g + 1) * BLOCKS)
                    high(g + 1, C_K)

                def high_values():
                    act.wait_ge(v_done, (g + 1) * BLOCKS)
                    high(g + 1, C_V)

                body(g * BLOCKS, 0, after_q=None if first else lambda h: h == REP - 1 and take_wo(g))
                body(g * BLOCKS + 1, 1, after_q=zero_points, after_k=high_keys)
                body(g * BLOCKS + 2, 2, after_q=lambda h: high(g + 1, C_Q + h), after_k=high_values)
                body(g * BLOCKS + 3, 3)

            take_wo(0)
            swap_k(0)
            for h in range(REP):
                swap_q(0, h)
            copy_vT(0)
            copy_scores(0)
            copy_v(0, 0)
            exps(0)
            swap_k(1)
            group(0, first=True)
            with act.Fori(1, KV_HEADS - 1) as g:
                group(g)
            base = (KV_HEADS - 1) * BLOCKS
            body(base, 0, after_q=lambda h: h == REP - 1 and take_wo(KV_HEADS - 1))
            body(base + 1, 1)
            body(base + 2, 2, last=True)

            catA = w_hi[:, 0:2048].rearrange("p (k g r) -> p k g r", k=KT, g=LGROUPS)
            catB = hT_hi[:, FB:FB + 4096].rearrange("p (g n) -> p g n", g=LGROUPS)
            copy_probT(STEPS - 1)
            context_hi(STEPS - 1)
            act.wait_ge(lora_in, 16 * LORA_LOADS)
            for k in range(KT):
                nc.scalar.activation(
                    catA[:, k, :, RANK:2 * RANK],
                    sharedA[:, k * RANK:(k + 1) * RANK].rearrange("p (g r) -> p g r", g=1).to_broadcast([P, LGROUPS, RANK]),
                    ACT.Identity).then_inc(lora_hi, 1)
            act.wait_ge(rest_ok, 2)
            for rows, src in ((slice(RANK, 2 * RANK), sharedB), (slice(2 * RANK, 2 * RANK + 1), bias_row)):
                nc.scalar.activation(catB[rows, :, :],
                                     src.rearrange("p (g n) -> p g n", g=1).to_broadcast([src.shape[0], LGROUPS, 512]),
                                     ACT.Identity).then_inc(lora_hi, 1)
            act.wait_ge(lora_pe, 1)
            for k in range(KT):
                src = (k_bank, t_bank)[k // 2][:, 256 * (k % 2):256 * (k % 2) + 256]
                nc.scalar.activation(catA[:, k, :, 0:RANK], src.rearrange("p (g r) -> p g r", g=LGROUPS),
                                     ACT.Identity).then_inc(lora_hi, 1)
            for j in range(2):
                act.wait_ge(lora_pe, 2 + j)
                for b in range(4):
                    nc.scalar.activation(catB[0:RANK, 4 * j + b, :], q_bank[j][b * RANK:(b + 1) * RANK, :],
                                         ACT.Identity).then_inc(lora_hi, 1)

            def copy_at(i):
                for s in range(2):
                    used(act, tx_done, 2 * i + s - 1)
                    nc.scalar.activation(ktn(at_sb[s]), turned_tile(2 * i + s), ACT.Identity).then_inc(at_ok, 1)

            def y_bias(i):
                for s in range(2):
                    act.wait_ge(y_done, 2 * i + s + 1)
                    used(act, yt_done, 2 * i)
                    nc.scalar.activation(y_sb[s], q_bank[s][:, :], ACT.Identity,
                                         bias=mbias[:, bass.ds(2 * i + s, 1)]).then_inc(y_ok, 1)

            def yT_high(i):
                for s in range(2):
                    act.wait_ge(yt_done, 2 * i + s + 1)
                    used(act, kern_used, 2 * i)
                    nc.scalar.activation(yT_all[0][s], q_bank[2 + s][:, :], ACT.Identity).then_inc(yT_hi_ok, 1)

            def ax_copy(i):
                for s in range(2):
                    act.wait_ge(ax_done, 2 * i + s + 1)
                    nc.scalar.activation(ax_sb[s][:, 0:2 * RANK], (s_bank, t_bank)[s][:, 0:2 * RANK],
                                         ACT.Identity).then_inc(ax_ok, 1)

            def axT_high(i):
                for s in range(2):
                    act.wait_ge(axt_done, 2 * i + s + 1)
                    nc.scalar.activation(axT[0][s], (s_bank, t_bank)[s][:, 128:256], ACT.Identity).then_inc(axT_hi_ok, 1)

            act.wait_ge(out_added, PARTS * STEPS)
            copy_at(0)
            act.wait_ge(lora_ok, 18)
            y_bias(0)
            yT_high(0)
            copy_at(1)
            ax_copy(0)

            def ffn_body(i, more=True):
                axT_high(i)
                y_bias(i + 1)
                yT_high(i + 1)
                if more:
                    copy_at(i + 2)
                ax_copy(i + 1)

            ffn_body(0)
            with act.Fori(1, TILES // 2 - 2) as i:
                ffn_body(i)
            ffn_body(TILES // 2 - 2, more=False)
            axT_high(TILES // 2 - 1)

        @block.vector
        def _(dve):
            for part in (ctx_hi, ctx_lo):
                for s in range(2):
                    for edge in (0, PAD + HID):
                        dve.memset(f32(part[:, s * XW + edge:s * XW + edge + PAD]), 0.0).then_inc(pads, 1)
            dve.wait_ge(con_in, 16 * (CONV_LOADS + 1))
            nc.vector.tensor_tensor(
                convw.rearrange("p (k j c) -> p k j c", k=TAPS, c=8),
                su["t72"].rearrange("p (k j c) -> p k j c", k=TAPS, j=1).to_broadcast([P, TAPS, 16, 8]),
                con[:, BD8:BD8 + 16].rearrange("p (k j c) -> p k j c", k=1, c=1).to_broadcast([P, TAPS, 16, 8]),
                ALU.mult).then_inc(convw_ok, 1)
            dve.wait_ge(convw_ok, 1)
            nc.vector.tensor_copy(convw_hi, convw).then_inc(convw_ok, 1)
            dve.wait_ge(convw_ok, 2)
            for tap, part in convw_lo:
                cols = slice(tap * 128, tap * 128 + part.shape[1])
                nc.vector.tensor_tensor(part, convw[:, cols], f32(convw_hi[:, cols]), ALU.subtract).then_inc(convw_ok, 1)

            def per_tile(ap, b):
                return ap[b * 32:(b + 1) * 32, :].rearrange("p (t b) -> p t b", b=BPT)[:, :, b]

            dve.wait_ge(su_pe, 1)
            for b in range(BPT):
                nc.vector.tensor_scalar(cbias[b * 32:(b + 1) * 32, :], per_tile(s_bank[:, 0:64], b),
                                        su["fb"][b * 32:(b + 1) * 32, :], None, ALU.add).then_inc(cbias_ok, 1)
            att, st = su["att"], stat[0:BATCH, :, 0:1]
            dve.wait_ge(su_pe, 4)
            nc.vector.tensor_tensor(att, s_bank[0:BATCH, 192:200], su["b2"], ALU.add).then_inc(su_dve, 1)
            dve.wait_ge(su_dve, 1)
            nc.vector.tensor_reduce(st[:, 0, :], att, AX_X, ALU.max).then_inc(su_dve, 1)
            dve.wait_ge(su_dve, 2)
            nc.vector.tensor_scalar(att, att, st[:, 0, :], None, ALU.subtract).then_inc(su_dve, 1)
            dve.wait_ge(su_act, 3)
            nc.vector.tensor_reduce(st[:, 1, :], att, AX_X, ALU.add).then_inc(su_dve, 1)
            dve.wait_ge(su_dve, 4)
            nc.vector.reciprocal(st[:, 2, :], st[:, 1, :]).then_inc(su_dve, 1)
            dve.wait_ge(su_dve, 5)
            nc.vector.tensor_scalar(att, att, st[:, 2, :], None, ALU.mult).then_inc(su_dve, 1)
            dve.wait_ge(su_pe, 5)
            nc.vector.tensor_copy(su["attT"], s_bank[0:MIX, 256:320]).then_inc(su_dve, 1)

            def split_x(t, s):
                xt = tile_of(t)
                mid = slice(PAD, PAD + HID)
                nc.vector.tensor_copy(x_hi[s][:, mid], xt).then_inc(x_hi_ok, 1)
                dve.wait_ge(x_hi_ok, t + 1)
                nc.vector.tensor_tensor(x_lo[s][:, mid], xt, f32(x_hi[s][:, mid]), ALU.subtract).then_inc(x_split, 1)

            def hT_low(t, s):
                dve.wait_ge(hT_hi_ok, t + 1)
                at = [part[:, :].rearrange("p (k t n) -> p k t n", k=KT, n=P)[:, :, bass.ds(t, 1), :]
                      for part in (hT_hi, hT_lo)]
                nc.vector.tensor_tensor(at[1], ktn(q_bank[2 + s][:, :]), f32(at[0]), ALU.subtract).then_inc(hT_ok, 1)

            dve.wait_ge(pads, 8)
            dve.wait_ge(x_in[0], 16)
            for s in range(2):
                split_x(s, s)
            dve.wait_ge(su_pe, 6)
            attR = su["attR"].rearrange("p (k t) -> p k t", k=MIX)
            for b in range(BPT):
                rows = slice(b * 32, (b + 1) * 32)
                nc.vector.tensor_copy(mbias[rows, :], per_tile(s_bank[:, 320:384], b)).then_inc(su_dve, 1)
                nc.vector.tensor_copy(attR[rows, :, :],
                                      t_bank[rows, :].rearrange("p (k t b) -> p k t b", k=MIX, b=BPT)[:, :, :, b])\
                    .then_inc(su_dve, 1)
            mixk = su["mixk"].rearrange("p (k o) -> p k o", k=MIX)
            prod = su["prod"].rearrange("p (t o) -> p t o", t=TILES)
            step = 7 + 2 * BPT
            for k in range(MIX):
                dve.wait_ge(su_dve, step)
                nc.vector.tensor_tensor(mixw[:, :, :] if k == 0 else prod,
                                        attR[:, k, :].rearrange("p (t o) -> p t o", o=1).to_broadcast([P, TILES, SEQ]),
                                        mixk[:, k:k + 1, :].to_broadcast([P, TILES, SEQ]), ALU.mult).then_inc(su_dve, 1)
                step += 1
                if k:
                    dve.wait_ge(su_dve, step)
                    nc.vector.tensor_tensor(mixw[:, :, :], mixw[:, :, :], prod, ALU.add).then_inc(su_dve, 1)
                    step += 1
            dve.wait_ge(su_dve, step)

            for q in range(1, 4):
                dve.wait_ge(x_in[q], 16)
            with dve.Fori(1, TILES // 2) as i:
                for s in range(2):
                    dve.wait_ge(conv_done, 2 * i + s - 1)
                    split_x(2 * i + s, s)
                for s in range(2):
                    hT_low(2 * i + s - 2, s)
            for s in range(2):
                hT_low(TILES - 2 + s, s)

            bq = "p (b q) -> p b q"

            def times_cos(j, src, signal):
                nc.vector.tensor_tensor(rope_c[j].rearrange(bq, b=BPB), src[:, :].rearrange(bq, b=BPB),
                                        cosT.rearrange(bq, b=1).to_broadcast([P, BPB, SEQ]), ALU.mult).then_inc(signal, 1)

            def cos_q(n, h):
                dve.wait_ge(q_swapped, 2 * (REP * n + h + 1))
                if h == 0:
                    dve.wait_ge(k_roped, n + 1)
                else:
                    used(dve, q_roped, REP * n + h - 1)
                times_cos(h % 2, q_bank[h], q_cos)

            def cos_k(n):
                dve.wait_ge(k_swapped, 2 * (n + 1))
                used(dve, q_roped, REP * n - 1)
                times_cos(0, k_bank, k_cos)

            pk = prob.rearrange("p (b k) -> p b k", b=BPB)

            def rows(j):
                return stat[:, j, :].rearrange("p (b o) -> p b o", o=1).to_broadcast([P, BPB, SEQ])

            def softmax_max(n):
                dve.wait_ge(turned, n + 1)
                used(dve, pt_done, n)
                nc.vector.tensor_tensor(pk, t_bank[:, :].rearrange("p (b k) -> p b k", b=BPB),
                                        limit.rearrange("p (b k) -> p b k", b=1).to_broadcast([P, BPB, SEQ]),
                                        ALU.min).then_inc(s_read, 1)
                dve.wait_ge(s_read, n + 1)
                nc.vector.tensor_reduce(stat[:, 0, :], pk, AX_X, ALU.max).then_inc(sm_step, 1)
                dve.wait_ge(sm_step, 5 * n + 1)
                nc.vector.tensor_tensor(pk, pk, rows(0), ALU.subtract).then_inc(sm_step, 1)

            def softmax_norm(n):
                dve.wait_ge(exp_done, n + 1)
                nc.vector.tensor_reduce(stat[:, 1, :], pk, AX_X, ALU.add).then_inc(sm_step, 1)
                dve.wait_ge(sm_step, 5 * n + 3)
                nc.vector.reciprocal(stat[:, 2, :], stat[:, 1, :]).then_inc(sm_step, 1)
                dve.wait_ge(sm_step, 5 * n + 4)
                nc.vector.tensor_tensor(pk, pk, rows(2), ALU.mult).then_inc(sm_step, 1)

            def context_lo(n):
                for r in range(BPT):
                    dve.wait_ge(ctx_hi_ok, BPT * n + r + 1)
                    nc.vector.tensor_tensor(context(ctx_lo, r), bank_thq(r), f32(context(ctx_hi, r)),
                                            ALU.subtract).then_inc(ctx_ok, 1)

            def add_out(n, g, blk, h, slices=range(KT)):
                for k in slices:
                    p = PARTS * n + KT * h + k
                    dve.wait_ge(out_done, p + 1)
                    used(dve, out_added, p - KT + 1)
                    at = acc[:, k * TOKENS + blk * BLOCK:k * TOKENS + (blk + 1) * BLOCK]
                    nc.vector.scalar_tensor_tensor(out=at, in0=(v_bank, s_bank)[k % 2][:, :],
                                                   scalar=wo_scale[:, bass.ds(g * PARTS + KT * h + k, 1)], in1=at,
                                                   op0=ALU.mult, op1=ALU.add).then_inc(out_added, 1)

            def body(n, prev=None):
                for h in range(REP):
                    if prev:
                        add_out(n - 1, *prev, h, (0, 1))
                    if h:
                        cos_q(n + 1, h - 1)
                    else:
                        cos_k(n + 1)
                    if prev:
                        add_out(n - 1, *prev, h, (2, 3))
                cos_q(n + 1, REP - 1)
                softmax_max(n + 1)
                context_lo(n)
                softmax_norm(n + 1)

            cos_k(0)
            for h in range(REP):
                cos_q(0, h)
            softmax_max(0)
            softmax_norm(0)
            body(0)
            dve.wait_ge(wo_scale_in, 16)
            dve.wait_ge(acc_zero, 1)
            for b in range(1, BLOCKS):
                body(b, (0, b - 1))
            with dve.Fori(1, KV_HEADS - 1) as g:
                body(g * BLOCKS, (g - 1, BLOCKS - 1))
                for b in range(1, BLOCKS):
                    body(g * BLOCKS + b, (g, b - 1))
            g = KV_HEADS - 1
            body(g * BLOCKS, (g - 1, BLOCKS - 1))
            for b in range(1, BLOCKS - 1):
                body(g * BLOCKS + b, (g, b - 1))
            for h in range(REP):
                add_out(STEPS - 2, g, BLOCKS - 2, h)
            dve.wait_ge(lora_in, 16 * LORA_LOADS)
            for k in range(4):
                nc.vector.tensor_tensor(
                    gsel[:, k * 256:(k + 1) * 256].rearrange("p (g r) -> p g r", g=LGROUPS),
                    gateT[:, k * 8:(k + 1) * 8].rearrange("p (g r) -> p g r", r=1).to_broadcast([P, LGROUPS, RANK]),
                    con[:, ID32:ID32 + RANK].rearrange("p (g r) -> p g r", g=1).to_broadcast([P, LGROUPS, RANK]),
                    ALU.mult).then_inc(gsel_ok, 1)
            context_lo(STEPS - 1)
            for h in range(REP):
                add_out(STEPS - 1, g, BLOCKS - 1, h)

            catA = [w[:, 0:2048].rearrange("p (k g r) -> p k g r", k=KT, g=LGROUPS) for w in (w_hi, w_lo)]
            catB = [w[:, FB:FB + 4096].rearrange("p (g n) -> p g n", g=LGROUPS) for w in (hT_hi, hT_lo)]
            for k in range(KT):
                dve.wait_ge(lora_hi, k + 1)
                nc.vector.tensor_tensor(
                    catA[1][:, k, :, RANK:2 * RANK],
                    sharedA[:, k * RANK:(k + 1) * RANK].rearrange("p (g r) -> p g r", g=1).to_broadcast([P, LGROUPS, RANK]),
                    f32(catA[0][:, k, :, RANK:2 * RANK]), ALU.subtract).then_inc(lora_ok, 1)
            for j, (rows_, src) in enumerate(((slice(RANK, 2 * RANK), sharedB),
                                              (slice(2 * RANK, 2 * RANK + 1), bias_row))):
                dve.wait_ge(lora_hi, KT + j + 1)
                nc.vector.tensor_tensor(catB[1][rows_, :, :],
                                        src.rearrange("p (g n) -> p g n", g=1).to_broadcast([src.shape[0], LGROUPS, 512]),
                                        f32(catB[0][rows_, :, :]), ALU.subtract).then_inc(lora_ok, 1)
            for k in range(KT):
                dve.wait_ge(lora_hi, KT + 2 + 2 * (k // 2) + 2)
                src = (k_bank, t_bank)[k // 2][:, 256 * (k % 2):256 * (k % 2) + 256]
                nc.vector.tensor_tensor(catA[1][:, k, :, 0:RANK], src.rearrange("p (g r) -> p g r", g=LGROUPS),
                                        f32(catA[0][:, k, :, 0:RANK]), ALU.subtract).then_inc(lora_ok, 1)
            for j in range(LGROUPS):
                dve.wait_ge(lora_hi, 2 * KT + 2 + j + 1)
                b = j % 4
                nc.vector.tensor_tensor(catB[1][0:RANK, j, :], q_bank[j // 4][b * RANK:(b + 1) * RANK, :],
                                        f32(catB[0][0:RANK, j, :]), ALU.subtract).then_inc(lora_ok, 1)

            def residual(i):
                dve.wait_ge(xs_in, 16 * i + 16)
                for s in range(2):
                    dve.wait_ge(tx_done, 2 * i + s + 1)
                    nc.vector.tensor_tensor(turned_tile(2 * i + s), ktn(q_bank[2 + s][:, :]),
                                            ktn(x_sb[:, 512 * s:512 * (s + 1)]), ALU.add).then_inc(x1_ok, 1)

            def yT_low(i):
                for s in range(2):
                    dve.wait_ge(yT_hi_ok, 2 * i + s + 1)
                    nc.vector.tensor_tensor(yT_all[1][s], q_bank[2 + s][:, :], f32(yT_all[0][s]),
                                            ALU.subtract).then_inc(yT_ok, 1)

            def axT_low(i):
                for s in range(2):
                    dve.wait_ge(axT_hi_ok, 2 * i + s + 1)
                    nc.vector.tensor_tensor(axT[1][s], (s_bank, t_bank)[s][:, 128:256], f32(axT[0][s]),
                                            ALU.subtract).then_inc(axT_ok, 1)

            def finish(i):
                for s in range(2):
                    dve.wait_ge(ffn_done, 2 * i + s + 1)
                    at = turned_tile(2 * i + s)
                    nc.vector.tensor_tensor(at, ktn((k_bank, v_bank)[s][:, :]), at, ALU.add).then_inc(result, 1)

            residual(0)
            yT_low(0)
            with dve.Fori(0, TILES // 2 - 1) as i:
                residual(i + 1)
                axT_low(i)
                yT_low(i + 1)
                finish(i)
            axT_low(TILES // 2 - 1)
            finish(TILES // 2 - 1)

        @block.tensor
        def _(pe):
            def three(dst, terms, start=True, stop=True):
                last = None
                for i, ((lh, ll), (rh, rl)) in enumerate(terms):
                    for j, (l, r) in enumerate(((lh, rh), (ll, rh), (lh, rl))):
                        last = nc.tensor.matmul(dst, l, r, start=start and i == 0 and j == 0,
                                                stop=stop and i == len(terms) - 1 and j == 2)
                return last

            def turn(dst, src):
                for k in range(4):
                    last = nc.tensor.transpose(dst[:, k * P:(k + 1) * P], src[:, k * P:(k + 1) * P], ident)
                return last

            pe.wait_ge(con_in, 16 * (CONV_LOADS + 1))
            nc.tensor.matmul(s_bank[:, 0:64], su["cwT"], su["condT"], start=True, stop=True).then_inc(su_pe, 1)
            pe.wait_ge(set_in, 16 * MLP_LOADS)
            nc.tensor.matmul(t_bank[:, 64:128], su["w0"], su["condT"], start=True, stop=True).then_inc(su_pe, 1)
            pe.wait_ge(cbias_ok, 4)
            pe.wait_ge(su_act, 1)
            nc.tensor.matmul(s_bank[:, 128:192], su["w1"], su["h1"], start=True, stop=True).then_inc(su_pe, 1)
            pe.wait_ge(su_act, 2)
            nc.tensor.matmul(s_bank[0:BATCH, 192:200], su["h2"], su["w2"], start=True, stop=True).then_inc(su_pe, 1)
            pe.wait_ge(su_dve, 6)
            nc.tensor.transpose(s_bank[0:MIX, 256:320], su["att"], ident[0:BATCH, 0:BATCH]).then_inc(su_pe, 1)
            pe.wait_ge(su_dve, 7)
            for k in range(MIX):
                nc.tensor.matmul(t_bank[:, k * 64:(k + 1) * 64], su["sel"][:, k * 128:(k + 1) * 128], su["attT"],
                                 start=True, stop=True)
            nc.tensor.matmul(s_bank[:, 320:384], su["biask"], su["attT"], start=True, stop=True).then_inc(su_pe, 1)

            pe.wait_ge(convw_ok, 4)

            def tap_lo(k):
                tap, part = convw_lo[k >= taps_in_wo]
                return part[:, (k - tap) * 128:(k - tap + 1) * 128]

            def conv_pair(i):
                for s in range(2):
                    pe.wait_ge(x_split, 2 * i + s + 1)
                    three(q_bank[s][:, :],
                          [((convw_hi[:, k * 128:(k + 1) * 128], tap_lo(k)),
                            (x_hi[s][:, k:k + HID], x_lo[s][:, k:k + HID])) for k in range(TAPS)]).then_inc(conv_done, 1)
                for s in range(2):
                    pe.wait_ge(h_ok, 2 * i + s + 1)
                    used(pe, hT_ok, 2 * i)
                    turn(q_bank[2 + s], h_tile[s]).then_inc(ht_done, 1)

            conv_pair(0)
            with pe.Fori(1, TILES // 2) as i:
                conv_pair(i)

            def project(dst, c, blk, slices=range(KT)):
                return three(dst[:, :], [((w_hi[:, c * 512 + k * P:c * 512 + (k + 1) * P],
                                           w_lo[:, c * 512 + k * P:c * 512 + (k + 1) * P]),
                                          (hT(hT_hi, k, blk * BLOCK, BLOCK), hT(hT_lo, k, blk * BLOCK, BLOCK)))
                                         for k in slices], start=slices[0] == 0, stop=slices[-1] == KT - 1)

            def keys(n, blk, g=None, slices=range(KT)):
                if g is not None:
                    pe.wait_ge(w_ready, g * CHUNKS + C_K + 1)
                used(pe, k_cos, n)
                last = project(k_bank, C_K, blk, slices)
                if slices[-1] == KT - 1:
                    last.then_inc(k_done, 1)

            def queries(h, blk, g=None, slices=range(KT)):
                if g is not None:
                    pe.wait_ge(w_ready, g * CHUNKS + C_Q + h + 1)
                last = project(q_bank[h], C_Q + h, blk, slices)
                if slices[-1] == KT - 1:
                    last.then_inc(q_done, 1)

            def values(n, blk, g=None):
                if g is not None:
                    pe.wait_ge(w_ready, g * CHUNKS + C_V + 1)
                used(pe, out_added, PARTS * (n - 1) - 1)
                project(v_bank, C_V, blk).then_inc(v_done, 1)

            def output(n, h, slices=range(KT)):
                for k in slices:
                    p = PARTS * n + KT * h + k
                    if h > 0 or k >= 2:
                        pe.wait_ge(out_added, p - 1)
                    w = wo[:, h * HID + k * P:h * HID + (k + 1) * P]
                    dst = (v_bank, s_bank)[k % 2][:, :]
                    nc.tensor.matmul(dst, w, ctx_hi[:, h * BLOCK:(h + 1) * BLOCK], start=True, stop=False)
                    nc.tensor.matmul(dst, w, ctx_lo[:, h * BLOCK:(h + 1) * BLOCK], start=False, stop=True)\
                        .then_inc(out_done, 1)

            def transpose_probs(n):
                pe.wait_ge(sm_step, 5 * n + 5)
                turn(t_bank, prob).then_inc(pt_done, 1)

            def context_of(n, s, tiles=range(TPB)):
                pe.wait_ge(probT_ok, n + 1)
                for t in tiles:
                    for r in range(BPT):
                        rows = slice(32 * r, 32 * r + 32)
                        product = nc.tensor.matmul(q_bank[r][:, t * P:(t + 1) * P], v_sb[s][rows, t * P:(t + 1) * P],
                                                probT[rows, t * P:(t + 1) * P], start=True, stop=True)
                        if t == TPB - 1:
                            product.then_inc(pv_done, 1)

            def scores(n):
                pe.wait_ge(q_roped, REP * (n + 1))
                pe.wait_ge(k_roped, n + 1)
                used(pe, out_added, PARTS * (n - 1))
                for b in range(BPB):
                    t, r = b // BPT, b % BPT
                    last = nc.tensor.matmul(s_bank[32 * r:32 * r + 32, t * P:(t + 1) * P],
                                            roped_k[:, b * SEQ:(b + 1) * SEQ], roped_q[:, b * P:(b + 1) * P],
                                            start=True, stop=True)
                last.then_inc(scores_done, 1)
                pe.wait_ge(vT_ok, n + 1)
                turn(t_bank, vT).then_inc(vt_done, 1)

            def turn_scores(n):
                pe.wait_ge(st_ok, n + 1)
                pe.wait_ge(v_ok, n + 1)
                turn(t_bank, scoreT).then_inc(turned, 1)

            def body(n, b, g, prev=True, first_out=False, last=False):
                nxt = g + 1 if b == BLOCKS - 1 else None
                for h in range(REP):
                    for half in ((0, 1), (2, 3)):
                        if prev:
                            pe.wait_ge(ctx_ok, BPT * (n - 1) + h + 1)
                        queries(h, (b + 1) % BLOCKS, nxt, half)
                        if prev:
                            pe.wait_ge(ctx_ok, BPT * n)
                            if first_out:
                                pe.wait_ge(wo_ready, g + 1)
                            output(n - 1, h, half)
                transpose_probs(n)
                next_keys = ((b + 2) % BLOCKS, g + 1 if b == BLOCKS - 2 else None)
                if not last:
                    keys(n + 2, *next_keys, (0,))
                values(n + 1, (b + 1) % BLOCKS, nxt)
                pe.wait_ge(q_cos, REP * (n + 2))
                context_of(n, b % 2, (0,))
                scores(n + 1)
                context_of(n, b % 2, (1,))
                turn_scores(n + 1)
                context_of(n, b % 2, (2, 3))
                if not last:
                    keys(n + 2, *next_keys, (1, 2, 3))

            pe.wait_ge(w_ready, CHUNKS)
            pe.wait_ge(hT_ok, TILES)
            pe.wait_ge(su_dve, 7 + 2 * BPT)
            keys(0, 0)
            for h in range(REP):
                queries(h, 0)
            values(0, 0)
            scores(0)
            turn_scores(0)
            keys(1, 1)
            for b in range(BLOCKS):
                body(b, b, 0, prev=b > 0, first_out=b == 1)
            with pe.Fori(1, KV_HEADS - 1) as g:
                for b in range(BLOCKS):
                    body(g * BLOCKS + b, b, g, first_out=b == 1)
            g = KV_HEADS - 1
            for b in range(BLOCKS - 1):
                body(g * BLOCKS + b, b, g, first_out=b == 1, last=b == BLOCKS - 2)
            pe.wait_ge(ctx_ok, BPT * (STEPS - 1))
            for h in range(REP):
                output(STEPS - 2, h)
            transpose_probs(STEPS - 1)
            context_of(STEPS - 1, (STEPS - 1) % 2)

            pe.wait_ge(gsel_ok, 4)
            pe.wait_ge(k_cos, STEPS)
            pe.wait_ge(probT_ok, STEPS)
            for k in range(KT):
                dst = (k_bank, t_bank)[k // 2][:, 256 * (k % 2):256 * (k % 2) + 256]
                for part in range(4):
                    last = nc.tensor.matmul(dst, loraA[:, part * 512 + k * P:part * 512 + (k + 1) * P],
                                            gsel[:, part * 256:(part + 1) * 256], start=part == 0, stop=part == 3)
            last.then_inc(lora_pe, 1)
            pe.wait_ge(ctx_ok, BPT * STEPS)
            for j in range(2):
                for part in range(4):
                    last = nc.tensor.matmul(q_bank[j][:, :],
                                            gsel[:, part * 256 + j * P:part * 256 + (j + 1) * P],
                                            loraB[:, part * 512:(part + 1) * 512], start=part == 0, stop=part == 3)
                last.then_inc(lora_pe, 1)
            for h in range(REP):
                output(STEPS - 1, h)

            pe.wait_ge(kern_ok, 1)
            pe.wait_ge(rest_ok, 6)

            def turn_back(i):
                for s in range(2):
                    pe.wait_ge(at_ok, 2 * i + s + 1)
                    used(pe, yT_ok, 2 * i)
                    turn(q_bank[2 + s], at_sb[s]).then_inc(tx_done, 1)

            def mix(i):
                for s in range(2):
                    pe.wait_ge(bd_ok, 2 * i + s + 1)
                    pe.wait_ge(x1_ok, 2 * i + s + 1)
                    nc.tensor.matmul(q_bank[s][:, :], mixbd[s], turned_tile(2 * i + s),
                                     start=True, stop=True).then_inc(y_done, 1)

            def transpose_y(i):
                for s in range(2):
                    pe.wait_ge(y_ok, 2 * i + s + 1)
                    turn(q_bank[2 + s], y_sb[s]).then_inc(yt_done, 1)

            def yT(s, k):
                return tuple(part[s][:, k * P:(k + 1) * P] for part in yT_all)

            def low_rank(i):
                for s in range(2):
                    pe.wait_ge(yT_ok, 2 * i + s + 1)
                    three((s_bank, t_bank)[s][:, 0:2 * RANK],
                          [(yT(s, k), tuple(w[:, bass.ds(i * 64 + k * 512, 64)] for w in (w_hi, w_lo)))
                           for k in range(KT)]).then_inc(ax_done, 1)

            def times_kernel(i, s):
                used(pe, result, 2 * i)
                three((k_bank, v_bank)[s][:, :],
                      [(yT(s, k), (hT_hi[:, FK + k * 512:FK + (k + 1) * 512],
                                   hT_lo[:, FK + k * 512:FK + (k + 1) * 512])) for k in range(KT)],
                      stop=False).then_inc(kern_used, 1)

            def transpose_ax(i):
                for s in range(2):
                    pe.wait_ge(ax_ok, 2 * i + s + 1)
                    nc.tensor.transpose((s_bank, t_bank)[s][:, 128:256], ax_sb[s], ident).then_inc(axt_done, 1)

            def low_rank_out(i):
                for s in range(2):
                    pe.wait_ge(axT_ok, 2 * i + s + 1)
                    three((k_bank, v_bank)[s][:, :],
                          [((axT[0][s], axT[1][s]),
                            (hT_hi[:, bass.ds(FB + i * 512, 512)], hT_lo[:, bass.ds(FB + i * 512, 512)]))],
                          start=False).then_inc(ffn_done, 1)

            turn_back(0)
            pe.wait_ge(lora_ok, 18)
            mix(0)
            transpose_y(0)
            low_rank(0)

            def ffn_body(i):
                turn_back(i + 1)
                times_kernel(i, 0)
                transpose_ax(i)
                mix(i + 1)
                times_kernel(i, 1)
                transpose_y(i + 1)
                low_rank_out(i)
                low_rank(i + 1)

            ffn_body(0)
            with pe.Fori(1, TILES // 2 - 1) as i:
                ffn_body(i)
            i = TILES // 2 - 1
            times_kernel(i, 0)
            transpose_ax(i)
            times_kernel(i, 1)
            low_rank_out(i)


def constants():
    import numpy as np
    con = np.zeros((P, CON_N), np.float32)
    p = np.arange(P)
    inv = (1.0 / np.float32(10000.0) ** (np.arange(0, HEAD, 2, dtype=np.float32) / np.float32(HEAD))).astype(np.float32)
    freq = np.arange(SEQ, dtype=np.float32)[:, None] * inv
    con[:, COS:COS + SEQ] = np.concatenate([np.cos(freq), np.cos(freq)], 1).T
    con[:, SIN:SIN + SEQ] = np.concatenate([-np.sin(freq), np.sin(freq)], 1).T
    big = np.finfo(np.float32)
    con[:, LIM:LIM + SEQ] = np.where(np.arange(SEQ)[None] <= (p % SEQ)[:, None], big.max, big.min)
    con[:, IDN:IDN + P] = np.eye(P, dtype=np.float32)
    con[:, BD8:BD8 + 16] = (p[:, None] // 8 == np.arange(16)[None])
    con[:, BD32:BD32 + BPT] = (p[:, None] // 32 == np.arange(BPT)[None])
    con[:, ID32:ID32 + 32] = (p[:, None] % 32 == np.arange(32)[None])
    sel = np.zeros((MIX, MIX, P), np.float32)
    for k in range(MIX):
        sel[k, k] = 1.0
    return con, sel.reshape(MIX, MIX * P)


def kernel(**inputs):
    import numpy as np
    import concourse.bacc as bacc
    from concourse import mybir as mb
    from concourse.bass_utils import run_bass_kernel_spmd

    i = {k: np.asarray(v) for k, v in inputs.items()}
    c = np.ascontiguousarray

    def proj(w):
        return w.reshape(KT, P, -1, P).transpose(2, 1, 0, 3).reshape(-1, P, 512)

    def srow(w):
        return w.reshape(KT, -1, P).transpose(1, 0, 2).reshape(-1, 512)

    def group(k, q, v):
        return c(np.concatenate([k[:, None], q.reshape(KV_HEADS, REP, *q.shape[1:]), v[:, None]], axis=1))

    con, sel = constants()
    arrays = {
        "con": con, "sel": sel,
        "x": c(i["x"].reshape(TILES, P, HID)),
        "condT": c(i["cond_128"].T),
        "fb": c(np.tile(i["fside_S_0"], BPT).reshape(P, 1)),
        "t72": c(np.tile(i["L0_cond_weight"].reshape(4, 8, 8, TAPS).transpose(0, 2, 3, 1).reshape(32, TAPS * 8), (BPT, 1))),
        "cwT": c(np.tile(i["L0_cond_c_weight"].T, (1, BPT))),
        "w0": c(i["L0_cond2_W0"]), "w1": c(i["L0_cond2_W1"]), "w2": c(i["L0_cond2_W2"]),
        "b0": c(i["L0_cond2_b0"].reshape(P, 1)), "b1": c(i["L0_cond2_b1"].reshape(P, 1)),
        "b2": c(i["L0_cond2_b2"].reshape(1, MIX)),
        "biask": c(np.tile(i["L0_cond2_bias_k"], (1, BPT))),
        "mixk": c(np.tile(i["L0_cond2_weight"][..., 0].transpose(2, 0, 1).reshape(32, MIX * 32), (BPT, 1))),
        "qw": group(proj(i["L0_attn_qw_k"]), proj(i["L0_attn_qw_q"]), proj(i["L0_attn_qw_v"])),
        "scales": group(srow(i["L0_attn_scales_k"]), srow(i["L0_attn_scales_q"]), srow(i["L0_attn_scales_v"])),
        "wo": c(i["L0_attn_qw_o"].reshape(KV_HEADS, REP, P, HID).transpose(0, 2, 1, 3).reshape(KV_HEADS, P, REP * HID)),
        "wo_scale": c(i["L0_attn_scales_o"].reshape(KV_HEADS * REP, KT, P).transpose(2, 0, 1).reshape(P, -1)),
        "kern": c(i["L0_ffn_kernel"].reshape(KT, P, 512).transpose(1, 0, 2)),
        "fbias": c(i["L0_ffn_bias"].reshape(1, HID)),
        "loraA": c(i["L0_ffn_lora_A"].reshape(4, P, 512).transpose(1, 0, 2)),
        "loraB": c(i["L0_ffn_lora_B"].transpose(0, 2, 1).reshape(4, P, 512).transpose(1, 0, 2)),
        "gateT": c(i["L0_ffn_gate"].T.reshape(4, 4, LGROUPS).transpose(1, 0, 2).reshape(4, 32)),
        "sharedA": c(i["L0_ffn_lora_A_shared"].T.reshape(KT, P, RANK).transpose(1, 0, 2).reshape(P, KT * RANK)),
        "sharedB": c(i["L0_ffn_lora_B_shared"].T),
    }
    nc = bacc.Bacc("TRN2", target_bir_lowering=False, num_devices=1)
    aps = {k: nc.dram_tensor(f"in_{k}", v.shape, mb.dt.from_np(v.dtype), kind="ExternalInput").ap()
           for k, v in arrays.items()}
    out = nc.dram_tensor("out_x", (TILES, P, HID), mb.dt.from_np(np.dtype("float32")), kind="ExternalOutput").ap()
    build(nc, aps, out)
    r = run_bass_kernel_spmd(nc, [{f"in_{k}": v for k, v in arrays.items()}], core_ids=[0])
    return r.results[0]["out_x"].reshape(BATCH, SEQ, HID)
```

```python
from contextlib import ExitStack

import concourse.bass as bass
from concourse import mybir

F32 = mybir.dt.float32
F32R = mybir.dt.float32r
I32 = mybir.dt.int32
ALU = mybir.AluOpType
ACT = mybir.ActivationFunctionType
AX_X = mybir.AxisListType.X

P = 128
BATCH, SEQ, HID = 64, 32, 512
TOKENS = BATCH * SEQ
TILES = TOKENS // P
BPT = P // SEQ
KT = HID // P
HEAD = 128
KV_HEADS = 8
REP = 4
BLOCK = 512
TPB = BLOCK // P
BPB = BLOCK // SEQ
BLOCKS = TOKENS // BLOCK
STEPS = KV_HEADS * BLOCKS
TAPS, PAD = 9, 4
XW = HID + 2 * PAD
FOLD = 4
FOLDS = -(-TAPS // FOLD)
RAW = 4
MIX = 8
NLORA, RANK = 16, 32
LGROUPS = 8
ZERO_POINT = 8.0

C_K, C_Q, C_V = 0, 1, 5
CHUNKS = 6
SCALED = 5
PARTS = REP * KT

COS, SIN, LIM, IDN, BDG, BD32, ID32, CON_N = 0, 32, 64, 96, 224, 228, 232, 264


def build(nc, a, out):
    ctx = ExitStack()
    with ctx:
        def sb(name, shape, dt=F32):
            return ctx.enter_context(nc.sbuf_tensor(name, shape, dt))

        def sem(name):
            return ctx.enter_context(nc.semaphore(name))

        bank = [ctx.enter_context(nc.psum_tensor(f"bank{i}", [P, 512], F32)) for i in range(8)]
        q_bank, k_bank, v_bank, s_bank, t_bank = bank[0:4], bank[4], bank[5], bank[6], bank[7]

        acc = sb("acc", [P, TILES * HID])
        hT_hi = sb("hT_hi", [P, KT * TOKENS], F32R)
        hT_lo = sb("hT_lo", [P, KT * TOKENS], F32R)
        w_hi = sb("w_hi", [P, CHUNKS * 512], F32R)
        w_lo = sb("w_lo", [P, SCALED * 512], F32R)
        w32 = sb("w32", [P, CHUNKS * 512])
        w_scale = sb("w_scale", [P, 2, 512])
        wo_land = sb("wo_land", [P, REP * HID])
        wo = sb("wo", [P, REP * HID], F32R)
        wo_scale = sb("wo_scale", [P, KV_HEADS * PARTS])
        v_scale = sb("v_scale", [P, KV_HEADS * KT])
        v_scale0 = sb("v_scale0", [P, 1])
        ctx_hi = sb("ctx_hi", [P, REP * BLOCK], F32R)
        ctx_lo = sb("ctx_lo", [P, REP * BLOCK], F32R)
        v_sb = [sb(f"v_sb{i}", [P, BLOCK])[:, :] for i in range(2)]
        work = sb("work", [P, 6656])
        con = sb("con", [P, CON_N])
        mixw = sb("mixw", [P, TILES, SEQ])
        cbias = sb("cbias", [P, TILES])
        mbias = sb("mbias", [P, TILES])
        stat = sb("stat", [P, 3, BPB])

        roped_q = work[:, 0:2048]
        rope_c = [work[:, 2048 + 1024 * j:2560 + 1024 * j] for j in range(2)]
        rope_s = [work[:, 2560 + 1024 * j:3072 + 1024 * j] for j in range(2)]
        roped_k = work[:, 4096:4608]
        vT = work[:, 4608:5120]
        scoreT = work[:, 5120:5632]
        prob = work[:, 5632:6144]
        probT = work[:, 6144:6656]

        cosT, sinT, limit = con[:, COS:COS + 32], con[:, SIN:SIN + 32], con[:, LIM:LIM + 32]
        ident = con[:, IDN:IDN + 128]

        h_tile = [work[:, 512 * s:512 * s + 512] for s in range(2)]
        o = 1024
        su = {}
        for name, rows, n in (("taps", P, FOLDS * 8), ("condT", P, BATCH), ("w0", P, 128), ("w1", P, 128),
                              ("w2", P, MIX), ("cwT", P, 128), ("b0", P, 1), ("b1", P, 1), ("fb", P, 1),
                              ("b2", BATCH, MIX), ("biask", MIX, 128), ("sel", MIX, MIX * 128),
                              ("mixk", P, MIX * 32), ("h1", P, BATCH), ("h2", P, BATCH), ("att", BATCH, MIX),
                              ("attT", MIX, BATCH), ("attR", P, MIX * TILES), ("prod", P, 512),
                              ("convw", P, FOLDS * 32)):
            su[name] = work[0:rows, o:o + n]
            o += n
        raw_in_work = 4096
        assert o <= raw_in_work
        convw = su["convw"]
        raw = [acc[:, r * BPT * XW:(r + 1) * BPT * XW] for r in range(RAW - 1)]
        raw.append(work[:, raw_in_work:raw_in_work + BPT * XW])
        loraA = wo_land[:, :]
        factorA = wo_land[:, :].rearrange("p (k g r) -> p k g r", k=KT, g=LGROUPS)
        loraB = w32[:, 0:2048]
        gateT = w32[:, 2048:2080]
        sharedA = w32[:, 2080:2208]
        sharedB = w32[32:64, 2208:2720]
        bias_row = w32[64:65, 2208:2720]
        gsel = w_scale[:, :, :].rearrange("p a b -> p (a b)")
        kern = work[:, 0:2048]
        factorB = work[0:RANK, 0:4096]
        at_sb = [work[:, 4096:4608], work[:, 5888:6400]]
        y_sb = v_sb
        x_sb = work[:, 4608:5632]
        mixbd = [work[:, 5632 + 128 * s:5760 + 128 * s] for s in range(2)]
        kern_parts = (hT_hi, hT_lo)
        outside = [w[:, 0:512] for w in (w_hi, w_lo)]
        inside = [w[:, 512:768] for w in (w_hi, w_lo)]
        low = [w[:, 768:1024] for w in (w_hi, w_lo)]
        yT = [w[:, 1024:2048] for w in (w_hi, w_lo)]

        con_in, set_in = sem("con_in"), sem("set_in")
        x_in = [sem(f"x_in{r}") for r in range(RAW)]
        su_pe, su_act, su_dve = sem("su_pe"), sem("su_act"), sem("su_dve")
        cbias_ok, convw_ok, pads = sem("cbias_ok"), sem("convw_ok"), sem("pads")
        mix_ok = sem("mix_ok")
        conv_done, h_ok, ht_done, hT_hi_ok, hT_ok = (sem(n) for n in
                                                     ("conv_done", "h_ok", "ht_done", "hT_hi_ok", "hT_ok"))
        w_in = [sem(f"w_in{c}") for c in range(CHUNKS)]
        scale_in = [sem(f"scale_in{s}") for s in range(2)]
        w_zeroed, w_scaled, w_hi_ok, w_ready = (sem(n) for n in ("w_zeroed", "w_scaled", "w_hi_ok", "w_ready"))
        wo_in, wo_ready, wo_scale_in = sem("wo_in"), sem("wo_ready"), sem("wo_scale_in")
        k_done, q_done, v_done = sem("k_done"), sem("q_done"), sem("v_done")
        k_swapped, k_cos, k_sin, k_roped = sem("k_swapped"), sem("k_cos"), sem("k_sin"), sem("k_roped")
        q_swapped, q_cos, q_sin, q_roped = sem("q_swapped"), sem("q_cos"), sem("q_sin"), sem("q_roped")
        wv_ready, v_scale_in, v_scale_ok = sem("wv_ready"), sem("v_scale_in"), sem("v_scale_ok")
        v_added, vt_done, v_ok = sem("v_added"), sem("vt_done"), sem("v_ok")
        scores_done, st_ok, turned, s_read = sem("scores_done"), sem("st_ok"), sem("turned"), sem("s_read")
        sm_step, exp_done = sem("sm_step"), sem("exp_done")
        pt_done, probT_ok, pv_done = sem("pt_done"), sem("probT_ok"), sem("pv_done")
        ctx_hi_ok, ctx_ok = sem("ctx_hi_ok"), sem("ctx_ok")
        out_done, out_added, acc_zero = sem("out_done"), sem("out_added"), sem("acc_zero")
        lora_in, kern_in, gsel_ok = sem("lora_in"), sem("kern_in"), sem("gsel_ok")
        lora_pe, lora_sb, shared_ok = sem("lora_pe"), sem("lora_sb"), sem("shared_ok")
        inside_hi_ok, inside_ok, outside_hi_ok, outside_ok = (sem(n) for n in ("inside_hi_ok", "inside_ok",
                                                                              "outside_hi_ok", "outside_ok"))
        kern_hi, kern_ok, rest_ok = sem("kern_hi"), sem("kern_ok"), sem("rest_ok")
        at_ok, tx_done, xs_in, x1_ok = sem("at_ok"), sem("tx_done"), sem("xs_in"), sem("x1_ok")
        bd_ok, y_done, y_ok, yt_done, yT_hi_ok, yT_ok = (sem(n) for n in
                                                         ("bd_ok", "y_done", "y_ok", "yt_done", "yT_hi_ok", "yT_ok"))
        low_done, low_hi_ok, low_ok = sem("low_done"), sem("low_hi_ok"), sem("low_ok")
        kern_used, ffn_done, result, stored = sem("kern_used"), sem("ffn_done"), sem("result"), sem("stored")

        CONV_LOADS, MLP_LOADS = 4, 9
        LORA_LOADS = 5 + P // RANK

        block = ctx.enter_context(nc.Block())

        def f32(ap):
            return ap.bitcast(F32)

        def hT(part, kt, tok0, n):
            return part[:, bass.ds(tok0 + kt * TOKENS, n)]

        def turned_tile(t):
            return acc[:, :].rearrange("p (k t n) -> p k t n", k=KT, n=P)[:, :, bass.ds(t, 1), :]

        def ktn(ap):
            return ap.rearrange("p (k t n) -> p k t n", k=KT, t=1)

        def used(eng, signal, count):
            if not isinstance(count, int) or count > 0:
                eng.wait_ge(signal, count)

        def context(part, r):
            return part[:, :].rearrange("p (h t b q) -> p t h b q", h=REP, t=TPB, b=BPT)[:, :, :, r, :]

        def bank_thq(r):
            return q_bank[r][:, :].rearrange("p (t h q) -> p t h q", t=TPB, h=REP)

        @block.sync
        def _(sp):
            sp.dma_start(con[:, :], a["con"]).then_inc(con_in, 16)
            for name in ("taps", "cwT", "condT", "fb"):
                sp.dma_start(su[name], a[name]).then_inc(con_in, 16)

            def load_tile(t, r):
                for tap in range(FOLD):
                    rows = raw[r][tap * SEQ:(tap + 1) * SEQ, :].rearrange("p (b n) -> p b n", b=BPT)
                    sp.dma_start(rows[:, :, PAD - tap:PAD - tap + HID],
                                 a["x"][bass.ds(t, 1), :, :].rearrange("t (b c) n -> c (t b) n", b=BPT)).then_inc(x_in[r], 16)

            sp.wait_ge(pads, 2 * RAW)
            load_tile(0, 0)
            load_tile(1, 1)
            for name in ("w0", "w1", "w2", "b0", "b1", "biask", "sel", "mixk"):
                sp.dma_start(su[name], a[name]).then_inc(set_in, 16)
            sp.dma_start(su["b2"], a["b2"].to_broadcast([BATCH, MIX])).then_inc(set_in, 16)

            load_tile(2, 2)
            load_tile(3, 3)

            def load(g, c):
                sp.dma_start(w32[:, c * 512:(c + 1) * 512].bitcast(I32),
                             a["qw"][g, c, :, :]).then_inc(w_in[c], 16)

            def load_scale(g, c):
                sp.dma_start(w_scale[:, c % 2, :],
                             a["scales"][g, c:c + 1, :].to_broadcast([P, 512])).then_inc(scale_in[c % 2], 16)

            def load_wo(g):
                sp.dma_start(wo_land[:, :].bitcast(I32), a["wo"][g, :, :]).then_inc(wo_in, 16)

            sp.dma_start(wo_scale[:, :], a["wo_scale"]).then_inc(wo_scale_in, 16)
            sp.dma_start(v_scale[:, :], a["v_scale"]).then_inc(v_scale_in, 16)

            def load_tiles(i):
                for r in range(RAW):
                    sp.wait_ge(conv_done, RAW * i + r - RAW + 1)
                    load_tile(RAW * i + r, r)

            load_tiles(1)
            for c in range(CHUNKS):
                load(0, c)
            for c in range(2):
                load_scale(0, c)
            with sp.Fori(2, TILES // RAW) as i:
                load_tiles(i)
            for c in range(2, SCALED):
                sp.wait_ge(w_scaled, c - 1)
                load_scale(0, c)
            load_wo(0)
            with sp.Fori(1, KV_HEADS) as g:
                for c in range(SCALED):
                    sp.wait_ge(w_ready, (g - 1) * SCALED + c + 1)
                    load(g, c)
                sp.wait_ge(wv_ready, g)
                load(g, C_V)
                for c in range(SCALED):
                    sp.wait_ge(w_scaled, g * SCALED + max(c - 1, 0))
                    load_scale(g, c)
                    if c == 1:
                        sp.wait_ge(wo_ready, g)
                        load_wo(g)
            sp.wait_ge(w_ready, KV_HEADS * SCALED)
            sp.wait_ge(wv_ready, KV_HEADS)
            sp.dma_start(loraB.rearrange("p (t n) -> p t n", t=4), a["loraB"]).then_inc(lora_in, 16)
            for q in range(P // RANK):
                sp.dma_start(gateT[q * RANK:(q + 1) * RANK, :],
                             a["gateT"][q:q + 1, :].to_broadcast([RANK, 32])).then_inc(lora_in, 16)
            sp.dma_start(sharedA, a["sharedA"]).then_inc(lora_in, 16)
            sp.dma_start(sharedB, a["sharedB"]).then_inc(lora_in, 16)
            sp.dma_start(bias_row, a["fbias"]).then_inc(lora_in, 16)
            sp.wait_ge(wo_ready, KV_HEADS)
            sp.dma_start(loraA.rearrange("p (t n) -> p t n", t=4), a["loraA"]).then_inc(lora_in, 16)
            sp.wait_ge(scores_done, STEPS)
            sp.dma_start(kern.rearrange("p (t n) -> p t n", t=KT), a["kern"]).then_inc(kern_in, 16)

            def load_x(i):
                sp.dma_start(x_sb.rearrange("p (t n) -> p t n", t=2),
                             a["x"][bass.ds(2 * i, 2), :, :].rearrange("t p n -> p t n")).then_inc(xs_in, 16)

            def store(i):
                sp.wait_ge(result, 2 * i + 2)
                for s in range(2):
                    sp.dma_start(out[bass.ds(2 * i + s, 1), :, :].rearrange("t p (k n) -> p k t n", k=KT),
                                 turned_tile(2 * i + s)).then_inc(stored, 16)

            sp.wait_ge(vt_done, STEPS)
            sp.wait_ge(turned, STEPS)
            load_x(0)
            sp.wait_ge(x1_ok, 2)
            load_x(1)
            with sp.Fori(0, TILES // 2 - 2) as i:
                sp.wait_ge(x1_ok, 2 * i + 4)
                load_x(i + 2)
                store(i)
            for i in range(TILES // 2 - 2, TILES // 2):
                store(i)
            sp.wait_ge(stored, 16 * TILES)

        @block.gpsimd
        def _(pool):
            def scale(g, c):
                w = w32[:, c * 512:(c + 1) * 512]
                pool.wait_ge(w_zeroed, g * SCALED + c + 1)
                pool.wait_ge(scale_in[c % 2], 16 * (g * (3 - c % 2) + c // 2 + 1))
                nc.gpsimd.tensor_tensor(w, w, w_scale[:, c % 2, :], ALU.mult).then_inc(w_scaled, 1)

            def split_low(g, c):
                sl = slice(c * 512, (c + 1) * 512)
                pool.wait_ge(w_hi_ok, g * SCALED + c + 1)
                nc.gpsimd.tensor_tensor(w_lo[:, sl], w32[:, sl], f32(w_hi[:, sl]), ALU.subtract).then_inc(w_ready, 1)

            sine = sinT.rearrange("p (b q) -> p b q", b=1).to_broadcast([P, BPB, SEQ])

            def add_q(n, h):
                i = REP * n + h
                s = rope_s[h % 2].rearrange("p (b q) -> p b q", b=BPB)
                pool.wait_ge(q_swapped, 2 * i + 2)
                nc.gpsimd.tensor_tensor(s, s, sine, ALU.mult).then_inc(q_sin, 1)
                pool.wait_ge(q_sin, i + 1)
                pool.wait_ge(q_cos, i + 1)
                used(pool, scores_done, n)
                nc.gpsimd.tensor_tensor(roped_q.rearrange("p (b h q) -> p b h q", b=BPB, h=REP)[:, :, h, :],
                                        rope_c[h % 2].rearrange("p (b q) -> p b q", b=BPB),
                                        s, ALU.add).then_inc(q_roped, 1)

            def add_k(n):
                s = rope_s[0].rearrange("p (b q) -> p b q", b=BPB)
                pool.wait_ge(k_swapped, 2 * n + 2)
                nc.gpsimd.tensor_tensor(s, s, sine, ALU.mult).then_inc(k_sin, 1)
                pool.wait_ge(k_sin, n + 1)
                pool.wait_ge(k_cos, n + 1)
                used(pool, scores_done, n)
                nc.gpsimd.tensor_tensor(roped_k, rope_c[0], rope_s[0], ALU.add).then_inc(k_roped, 1)

            def body(n, after_q=None, before_k=None, after_k=None, last=False):
                for h in range(REP):
                    add_q(n + 1, h)
                    if after_q and h != REP - 2:
                        for j in ((h,) if h < REP - 2 else (REP - 2, REP - 1)):
                            after_q(j)
                if before_k:
                    before_k()
                if not last:
                    add_k(n + 2)
                if after_k:
                    after_k()

            def group(g, first=False):
                def last_scales():
                    for c in range(REP, SCALED):
                        scale(g + 1, c)
                    if first:
                        clear(2)
                        clear(3)

                body(g * BLOCKS, after_k=(lambda: clear(1)) if first else None)
                body(g * BLOCKS + 1, after_q=lambda h: scale(g + 1, h), before_k=last_scales,
                     after_k=lambda: split_low(g + 1, C_K))
                body(g * BLOCKS + 2, after_q=lambda h: split_low(g + 1, C_Q + h))
                body(g * BLOCKS + 3)

            for c in range(SCALED):
                scale(0, c)
            for c in range(SCALED):
                split_low(0, c)
            add_k(0)
            for h in range(REP):
                add_q(0, h)
            add_k(1)

            def clear(b):
                nc.gpsimd.memset(acc[:, :].rearrange("p (k b n) -> p k b n", k=KT, b=BLOCKS)[:, :, b:b + 1, :],
                                 0.0).then_inc(acc_zero, 1)

            pool.wait_ge(conv_done, TILES)
            clear(0)
            group(0, first=True)
            with pool.Fori(1, KV_HEADS - 1) as g:
                group(g)
            base = (KV_HEADS - 1) * BLOCKS
            body(base)
            body(base + 1)
            pool.wait_ge(lora_in, 16 * LORA_LOADS)
            for k in range(4):
                nc.gpsimd.tensor_tensor(
                    gsel[:, k * 256:(k + 1) * 256].rearrange("p (g r) -> p g r", g=LGROUPS),
                    gateT[:, k * 8:(k + 1) * 8].rearrange("p (g r) -> p g r", r=1).to_broadcast([P, LGROUPS, RANK]),
                    con[:, ID32:ID32 + RANK].rearrange("p (g r) -> p g r", g=1).to_broadcast([P, LGROUPS, RANK]),
                    ALU.mult).then_inc(gsel_ok, 1)
            body(base + 2, last=True)

            rest = slice(2 * RANK, P)
            pool.wait_ge(v_done, KT * STEPS)
            pool.wait_ge(q_roped, REP * STEPS)
            for place in (*outside, *low):
                nc.gpsimd.memset(f32(place[rest, :]), 0.0).then_inc(rest_ok, 1)
            pool.wait_ge(rest_ok, 4)
            nc.gpsimd.memset(f32(low[0][2 * RANK:2 * RANK + 1, :]), 1.0).then_inc(rest_ok, 1)
            pool.wait_ge(rest_ok, 5)
            pool.wait_ge(kern_in, 16)
            nc.gpsimd.tensor_copy(hT_hi[:, 0:2048], kern).then_inc(kern_hi, 1)
            pool.wait_ge(kern_hi, 1)
            nc.gpsimd.tensor_tensor(hT_lo[:, 0:2048], kern, f32(hT_hi[:, 0:2048]), ALU.subtract).then_inc(kern_ok, 1)

            def slices(ap):
                return ap.rearrange("p (k g r) -> p k g r", k=KT, g=1)

            def inside_low(i):
                pool.wait_ge(inside_hi_ok, i + 1)
                nc.gpsimd.tensor_tensor(slices(inside[1]), factorA[:, :, bass.ds(i, 1), :],
                                        slices(f32(inside[0])), ALU.subtract).then_inc(inside_ok, 1)

            def outside_low(i):
                pool.wait_ge(outside_hi_ok, i + 1)
                pool.wait_ge(inside_ok, i + 1)
                nc.gpsimd.tensor_tensor(outside[1][0:RANK, :], factorB[:, bass.ds(i * 512, 512)],
                                        f32(outside[0][0:RANK, :]), ALU.subtract).then_inc(outside_ok, 1)

            def block_diagonal(t, s):
                nc.gpsimd.tensor_tensor(
                    mixbd[s].rearrange("p (b o) -> p b o", b=BPT),
                    mixw[:, bass.ds(t, 1), :].to_broadcast([P, BPT, SEQ]),
                    con[:, BD32:BD32 + BPT].rearrange("p (b o) -> p b o", o=1).to_broadcast([P, BPT, SEQ]),
                    ALU.mult).then_inc(bd_ok, 1)

            pool.wait_ge(mix_ok, 2 * MIX - 1)
            pool.wait_ge(pt_done, STEPS)
            for s in range(2):
                block_diagonal(s, s)
            inside_low(0)
            outside_low(0)
            with pool.Fori(1, TILES // 2) as i:
                pool.wait_ge(outside_ok, i)
                for s in range(2):
                    pool.wait_ge(y_done, 2 * i + s - 1)
                    block_diagonal(2 * i + s, s)
                inside_low(i)
                outside_low(i)

        @block.scalar
        def _(act):
            def zero_point(g, c):
                w = w32[:, c * 512:(c + 1) * 512]
                act.wait_ge(w_in[c], 16 * (g + 1))
                nc.scalar.activation(w, w.bitcast(I32), ACT.Copy, bias=-ZERO_POINT).then_inc(w_zeroed, 1)

            def high(g, c):
                sl = slice(c * 512, (c + 1) * 512)
                act.wait_ge(w_scaled, g * SCALED + c + 1)
                nc.scalar.activation(w_hi[:, sl], w32[:, sl], ACT.Identity).then_inc(w_hi_ok, 1)

            def take_wv(g):
                act.wait_ge(w_in[C_V], 16 * (g + 1))
                sl = slice(C_V * 512, (C_V + 1) * 512)
                nc.scalar.activation(w_hi[:, sl], w32[:, sl].bitcast(I32), ACT.Copy, bias=-ZERO_POINT).then_inc(wv_ready, 1)
                nc.scalar.activation(v_scale0[:, :], v_scale[:, bass.ds(g * KT, 1)], ACT.Identity).then_inc(v_scale_ok, 1)

            def take_wo(g):
                act.wait_ge(wo_in, 16 * (g + 1))
                used(act, out_done, PARTS * BLOCKS * g)
                nc.scalar.activation(wo[:, :], wo_land[:, :].bitcast(I32), ACT.Copy, bias=-ZERO_POINT).then_inc(wo_ready, 1)

            def gelu_1():
                act.wait_ge(su_pe, 2)
                nc.scalar.activation(su["h1"], t_bank[:, 64:128], ACT.Gelu, bias=su["b0"]).then_inc(su_act, 1)

            def gelu_2():
                act.wait_ge(su_pe, 3)
                nc.scalar.activation(su["h2"], s_bank[:, 128:192], ACT.Gelu, bias=su["b1"]).then_inc(su_act, 1)

            def exp_att():
                act.wait_ge(su_dve, 3)
                nc.scalar.activation(su["att"], su["att"], ACT.Exp).then_inc(su_act, 1)

            def bias_h(t, s):
                act.wait_ge(conv_done, t + 1)
                act.wait_ge(cbias_ok, 4)
                used(act, ht_done, t - 1)
                nc.scalar.activation(h_tile[s], q_bank[s][:, :], ACT.Identity,
                                     bias=cbias[:, bass.ds(t, 1)]).then_inc(h_ok, 1)

            def hT_high(t, s):
                act.wait_ge(ht_done, t + 1)
                nc.scalar.activation(
                    hT_hi[:, :].rearrange("p (k t n) -> p k t n", k=KT, n=P)[:, :, bass.ds(t, 1), :],
                    ktn(q_bank[2 + s][:, :]), ACT.Identity).then_inc(hT_hi_ok, 1)

            def four_tiles(i, between=()):
                for r in range(RAW):
                    bias_h(RAW * i + r, r % 2)
                    if r or not isinstance(i, int) or i:
                        hT_high(RAW * i + r - 1, (r - 1) % 2)
                    if r < len(between):
                        between[r]()

            four_tiles(0, (gelu_1, gelu_2))
            four_tiles(1, (exp_att,))
            four_tiles(2, [lambda c=c: zero_point(0, c) for c in range(RAW)])
            zero_point(0, SCALED - 1)
            act.wait_ge(v_scale_in, 16)
            take_wv(0)
            four_tiles(3, [lambda c=c: high(0, c) for c in range(RAW)])
            high(0, SCALED - 1)
            hT_high(TILES - 1, 1)

            def swap(dst, src, signal):
                for to, fro in ((0, 64), (64, 0)):
                    nc.scalar.activation(dst[to:to + 64, :], src[fro:fro + 64, :], ACT.Identity).then_inc(signal, 1)

            def swap_q(n, h):
                act.wait_ge(q_done, REP * n + h + 1)
                if h == 0:
                    act.wait_ge(k_roped, n + 1)
                else:
                    used(act, q_roped, REP * n + h - 1)
                swap(rope_s[h % 2], q_bank[h], q_swapped)

            def swap_k(n):
                act.wait_ge(k_done, n + 1)
                used(act, q_roped, REP * n - 1)
                swap(rope_s[0], k_bank, k_swapped)

            def first_v(n, g):
                act.wait_ge(v_done, KT * n + 1)
                used(act, vt_done, n)
                act.wait_ge(v_scale_ok, g + 1)
                nc.scalar.activation(vT, s_bank[:, :], ACT.Copy, scale=v_scale0[:, :]).then_inc(v_added, 1)

            def copy_v(n, s):
                act.wait_ge(vt_done, n + 1)
                used(act, pv_done, BPT * (n - 1))
                nc.scalar.activation(v_sb[s], t_bank[:, :], ACT.Identity).then_inc(v_ok, 1)

            def copy_scores(n):
                act.wait_ge(scores_done, n + 1)
                used(act, turned, n)
                nc.scalar.activation(scoreT, s_bank[:, :], ACT.Identity).then_inc(st_ok, 1)

            def exps(n):
                act.wait_ge(sm_step, 5 * n + 2)
                nc.scalar.activation(prob, prob, ACT.Exp, scale=HEAD ** -0.5).then_inc(exp_done, 1)

            def copy_probT(n):
                act.wait_ge(pt_done, n + 1)
                nc.scalar.activation(probT, t_bank[:, :], ACT.Identity).then_inc(probT_ok, 1)

            def context_hi(n):
                used(act, out_done, PARTS * n)
                for r in range(BPT):
                    act.wait_ge(pv_done, BPT * n + r + 1)
                    nc.scalar.activation(context(ctx_hi, r), bank_thq(r), ACT.Identity).then_inc(ctx_hi_ok, 1)

            def body(n, b, g, after_q=None, after_k=None, last=False):
                for h in range(REP):
                    swap_q(n + 1, h)
                    if h == REP - 1:
                        copy_probT(n)
                        first_v(n + 1, g + (b + 1) // BLOCKS)
                    if after_q:
                        after_q(h)
                copy_scores(n + 1)
                context_hi(n)
                copy_v(n + 1, (b + 1) % 2)
                if not last:
                    swap_k(n + 2)
                exps(n + 1)
                if after_k:
                    after_k()

            def group(g, first=False):
                def zero_points(h):
                    for c in ((0, 1), (2,), (3,), (4,))[h]:
                        zero_point(g + 1, c)

                def high_keys():
                    act.wait_ge(k_done, (g + 1) * BLOCKS)
                    high(g + 1, C_K)

                def next_values():
                    act.wait_ge(v_done, (g + 1) * BLOCKS * KT)
                    take_wv(g + 1)

                body(g * BLOCKS, 0, g, after_q=None if first else lambda h: h == REP - 1 and take_wo(g))
                body(g * BLOCKS + 1, 1, g, after_q=zero_points, after_k=high_keys)
                body(g * BLOCKS + 2, 2, g, after_q=lambda h: high(g + 1, C_Q + h), after_k=next_values)
                body(g * BLOCKS + 3, 3, g)

            take_wo(0)
            swap_k(0)
            first_v(0, 0)
            for h in range(REP):
                swap_q(0, h)
            copy_scores(0)
            copy_v(0, 0)
            exps(0)
            swap_k(1)
            group(0, first=True)
            with act.Fori(1, KV_HEADS - 1) as g:
                group(g)
            base = (KV_HEADS - 1) * BLOCKS
            body(base, 0, KV_HEADS - 1, after_q=lambda h: h == REP - 1 and take_wo(KV_HEADS - 1))
            body(base + 1, 1, KV_HEADS - 1)
            body(base + 2, 2, KV_HEADS - 1, last=True)

            copy_probT(STEPS - 1)
            act.wait_ge(lora_in, 16 * LORA_LOADS)
            act.wait_ge(rest_ok, 5)
            for rows, src in ((slice(RANK, 2 * RANK), sharedB), (slice(2 * RANK, 2 * RANK + 1), bias_row)):
                nc.scalar.activation(outside[0][rows, :], src, ACT.Identity).then_inc(lora_sb, 1)
            context_hi(STEPS - 1)
            act.wait_ge(lora_pe, 1)
            for k in range(KT):
                src = (k_bank, t_bank)[k // 2][:, 256 * (k % 2):256 * (k % 2) + 256]
                nc.scalar.activation(factorA[:, k, :, 0:RANK], src.rearrange("p (g r) -> p g r", g=LGROUPS),
                                     ACT.Identity).then_inc(lora_sb, 1)
                nc.scalar.activation(
                    factorA[:, k, :, RANK:2 * RANK],
                    sharedA[:, k * RANK:(k + 1) * RANK].rearrange("p (g r) -> p g r", g=1).to_broadcast([P, LGROUPS, RANK]),
                    ACT.Identity).then_inc(lora_sb, 1)

            def inside_high(i):
                used(act, low_done, i)
                nc.scalar.activation(inside[0].rearrange("p (k g r) -> p k g r", k=KT, g=1),
                                     factorA[:, :, bass.ds(i, 1), :], ACT.Identity).then_inc(inside_hi_ok, 1)

            def outside_high(i):
                used(act, ffn_done, 2 * i)
                nc.scalar.activation(outside[0][0:RANK, :], factorB[:, bass.ds(i * 512, 512)],
                                     ACT.Identity).then_inc(outside_hi_ok, 1)

            def copy_at(i):
                for s in range(2):
                    used(act, tx_done, 2 * i + s - 1)
                    nc.scalar.activation(ktn(at_sb[s]), turned_tile(2 * i + s), ACT.Identity).then_inc(at_ok, 1)

            def y_bias(i):
                for s in range(2):
                    act.wait_ge(y_done, 2 * i + s + 1)
                    used(act, yt_done, 2 * i)
                    nc.scalar.activation(y_sb[s], q_bank[s][:, :], ACT.Identity,
                                         bias=mbias[:, bass.ds(2 * i + s, 1)]).then_inc(y_ok, 1)

            def yT_high(i):
                for s in range(2):
                    act.wait_ge(yt_done, 2 * i + s + 1)
                    used(act, kern_used, 2 * i + s - 1)
                    nc.scalar.activation(yT[0].rearrange("p (k t n) -> p k t n", k=KT, t=2)[:, :, s:s + 1, :],
                                         ktn(q_bank[2 + s][:, :]), ACT.Identity).then_inc(yT_hi_ok, 1)

            def low_high(i):
                act.wait_ge(low_done, i + 1)
                used(act, ffn_done, 2 * i)
                nc.scalar.activation(low[0][0:2 * RANK, :], s_bank[0:2 * RANK, 0:256], ACT.Identity).then_inc(low_hi_ok, 1)

            act.wait_ge(lora_sb, 2 + 2 * KT)
            inside_high(0)
            act.wait_ge(out_added, PARTS * (STEPS - BLOCKS + 1))
            copy_at(0)
            act.wait_ge(kern_ok, 1)
            for j in range(2):
                act.wait_ge(lora_pe, 2 + j)
                for b in range(4):
                    nc.scalar.activation(factorB[:, (4 * j + b) * 512:(4 * j + b + 1) * 512],
                                         q_bank[j][b * RANK:(b + 1) * RANK, :], ACT.Identity).then_inc(lora_sb, 1)
            act.wait_ge(lora_sb, 2 + 2 * KT + LGROUPS)
            outside_high(0)
            y_bias(0)
            yT_high(0)
            act.wait_ge(out_added, PARTS * STEPS)
            copy_at(1)
            low_high(0)

            def ffn_body(i, more=True):
                if more:
                    copy_at(i + 2)
                inside_high(i + 1)
                y_bias(i + 1)
                yT_high(i + 1)
                outside_high(i + 1)
                low_high(i + 1)

            ffn_body(0)
            with act.Fori(1, TILES // 2 - 2) as i:
                ffn_body(i)
            ffn_body(TILES // 2 - 2, more=False)

        @block.vector
        def _(dve):
            for place in raw:
                rows_ = place.rearrange("p (b n) -> p b n", b=BPT)
                dve.memset(rows_[:, :, 0:PAD], 0.0).then_inc(pads, 1)
                dve.memset(rows_[:, :, HID:XW], 0.0).then_inc(pads, 1)
            dve.wait_ge(con_in, 16 * (CONV_LOADS + 1))
            nc.vector.tensor_tensor(
                convw.rearrange("p (k j c) -> p k j c", k=FOLDS, c=8),
                su["taps"].rearrange("p (k j c) -> p k j c", k=FOLDS, j=1).to_broadcast([P, FOLDS, 4, 8]),
                con[:, BDG:BDG + 4].rearrange("p (k j c) -> p k j c", k=1, c=1).to_broadcast([P, FOLDS, 4, 8]),
                ALU.mult).then_inc(convw_ok, 1)

            def per_tile(ap, b):
                return ap[b * 32:(b + 1) * 32, :].rearrange("p (t b) -> p t b", b=BPT)[:, :, b]

            dve.wait_ge(su_pe, 1)
            for b in range(BPT):
                nc.vector.tensor_scalar(cbias[b * 32:(b + 1) * 32, :], per_tile(s_bank[:, 0:64], b),
                                        su["fb"][b * 32:(b + 1) * 32, :], None, ALU.add).then_inc(cbias_ok, 1)

            def hT_low(t, s):
                dve.wait_ge(hT_hi_ok, t + 1)
                at = [part[:, :].rearrange("p (k t n) -> p k t n", k=KT, n=P)[:, :, bass.ds(t, 1), :]
                      for part in (hT_hi, hT_lo)]
                nc.vector.tensor_tensor(at[1], ktn(q_bank[2 + s][:, :]), f32(at[0]), ALU.subtract).then_inc(hT_ok, 1)

            att, st = su["att"], stat[0:BATCH, :, 0:1]

            def att_less_max():
                dve.wait_ge(su_pe, 4)
                nc.vector.tensor_tensor(att, s_bank[0:BATCH, 192:200], su["b2"], ALU.add).then_inc(su_dve, 1)
                dve.wait_ge(su_dve, 1)
                nc.vector.tensor_reduce(st[:, 0, :], att, AX_X, ALU.max).then_inc(su_dve, 1)
                dve.wait_ge(su_dve, 2)
                nc.vector.tensor_scalar(att, att, st[:, 0, :], None, ALU.subtract).then_inc(su_dve, 1)

            def att_rows():
                dve.wait_ge(su_act, 3)
                nc.vector.tensor_reduce(st[:, 1, :], att, AX_X, ALU.add).then_inc(su_dve, 1)
                dve.wait_ge(su_dve, 4)
                nc.vector.reciprocal(st[:, 2, :], st[:, 1, :]).then_inc(su_dve, 1)
                dve.wait_ge(su_dve, 5)
                nc.vector.tensor_scalar(att, att, st[:, 2, :], None, ALU.mult).then_inc(su_dve, 1)
                dve.wait_ge(su_pe, 5)
                nc.vector.tensor_copy(su["attT"], s_bank[0:MIX, 256:320]).then_inc(su_dve, 1)
                dve.wait_ge(su_pe, 6)
                attR = su["attR"].rearrange("p (k t) -> p k t", k=MIX)
                for b in range(BPT):
                    rows = slice(b * 32, (b + 1) * 32)
                    nc.vector.tensor_copy(mbias[rows, :], per_tile(s_bank[:, 320:384], b)).then_inc(su_dve, 1)
                    nc.vector.tensor_copy(attR[rows, :, :],
                                          t_bank[rows, :].rearrange("p (k t b) -> p k t b", k=MIX, b=BPT)[:, :, :, b])\
                        .then_inc(su_dve, 1)

            def mix_weights(*kernels):
                attR = su["attR"].rearrange("p (k t) -> p k t", k=MIX)
                mixk = su["mixk"].rearrange("p (k o) -> p k o", k=MIX)
                prod = su["prod"].rearrange("p (t o) -> p t o", t=TILES)
                dve.wait_ge(su_dve, 7 + 2 * BPT)
                for k in kernels:
                    used(dve, mix_ok, 2 * k - 1)
                    nc.vector.tensor_tensor(mixw[:, :, :] if k == 0 else prod,
                                            attR[:, k, :].rearrange("p (t o) -> p t o", o=1).to_broadcast([P, TILES, SEQ]),
                                            mixk[:, k:k + 1, :].to_broadcast([P, TILES, SEQ]), ALU.mult).then_inc(mix_ok, 1)
                    if k:
                        dve.wait_ge(mix_ok, 2 * k)
                        nc.vector.tensor_tensor(mixw[:, :, :], mixw[:, :, :], prod, ALU.add).then_inc(mix_ok, 1)

            def four_tiles(i, between=()):
                for r in range(RAW):
                    if r or not isinstance(i, int) or i:
                        hT_low(RAW * i + r - 1, (r - 1) % 2)
                    if r < len(between):
                        between[r]()

            four_tiles(0, (lambda: None, lambda: None, lambda: None, att_less_max))
            four_tiles(1, (lambda: None, att_rows, lambda: mix_weights(0, 1), lambda: mix_weights(2, 3)))
            four_tiles(2, (lambda: mix_weights(4, 5), lambda: mix_weights(6, 7)))
            four_tiles(3)
            hT_low(TILES - 1, 1)

            bq = "p (b q) -> p b q"

            def times_cos(j, src, signal):
                nc.vector.tensor_tensor(rope_c[j].rearrange(bq, b=BPB), src[:, :].rearrange(bq, b=BPB),
                                        cosT.rearrange(bq, b=1).to_broadcast([P, BPB, SEQ]), ALU.mult).then_inc(signal, 1)

            def cos_q(n, h):
                dve.wait_ge(q_swapped, 2 * (REP * n + h + 1))
                if h == 0:
                    dve.wait_ge(k_roped, n + 1)
                else:
                    used(dve, q_roped, REP * n + h - 1)
                times_cos(h % 2, q_bank[h], q_cos)

            def cos_k(n):
                dve.wait_ge(k_swapped, 2 * (n + 1))
                used(dve, q_roped, REP * n - 1)
                times_cos(0, k_bank, k_cos)

            pk = prob.rearrange("p (b k) -> p b k", b=BPB)

            def rows(j):
                return stat[:, j, :].rearrange("p (b o) -> p b o", o=1).to_broadcast([P, BPB, SEQ])

            def softmax_max(n):
                dve.wait_ge(turned, n + 1)
                used(dve, pt_done, n)
                nc.vector.tensor_tensor(pk, t_bank[:, :].rearrange("p (b k) -> p b k", b=BPB),
                                        limit.rearrange("p (b k) -> p b k", b=1).to_broadcast([P, BPB, SEQ]),
                                        ALU.min).then_inc(s_read, 1)
                dve.wait_ge(s_read, n + 1)
                nc.vector.tensor_reduce(stat[:, 0, :], pk, AX_X, ALU.max).then_inc(sm_step, 1)

            def softmax_less_max(n):
                dve.wait_ge(sm_step, 5 * n + 1)
                nc.vector.tensor_tensor(pk, pk, rows(0), ALU.subtract).then_inc(sm_step, 1)

            def softmax_sum(n):
                dve.wait_ge(exp_done, n + 1)
                nc.vector.tensor_reduce(stat[:, 1, :], pk, AX_X, ALU.add).then_inc(sm_step, 1)

            def softmax_norm(n):
                dve.wait_ge(sm_step, 5 * n + 3)
                nc.vector.reciprocal(stat[:, 2, :], stat[:, 1, :]).then_inc(sm_step, 1)
                dve.wait_ge(sm_step, 5 * n + 4)
                nc.vector.tensor_tensor(pk, pk, rows(2), ALU.mult).then_inc(sm_step, 1)

            def context_lo(n):
                for r in range(BPT):
                    dve.wait_ge(ctx_hi_ok, BPT * n + r + 1)
                    nc.vector.tensor_tensor(context(ctx_lo, r), bank_thq(r), f32(context(ctx_hi, r)),
                                            ALU.subtract).then_inc(ctx_ok, 1)

            def add_out(n, g, blk, h, slices=range(KT)):
                for k in slices:
                    p = PARTS * n + KT * h + k
                    dve.wait_ge(out_done, p + 1)
                    used(dve, out_added, p - KT + 1)
                    at = acc[:, k * TOKENS + blk * BLOCK:k * TOKENS + (blk + 1) * BLOCK]
                    nc.vector.scalar_tensor_tensor(out=at, in0=(v_bank, s_bank)[k % 2][:, :],
                                                   scalar=wo_scale[:, bass.ds(g * PARTS + KT * h + k, 1)], in1=at,
                                                   op0=ALU.mult, op1=ALU.add).then_inc(out_added, 1)

            def scale_v(n, g):
                for k in range(1, KT):
                    i = KT * n + k
                    dve.wait_ge(v_done, i + 1)
                    dve.wait_ge(v_added, i)
                    nc.vector.scalar_tensor_tensor(out=vT, in0=(s_bank, v_bank)[k % 2][:, :],
                                                   scalar=v_scale[:, bass.ds(g * KT + k, 1)], in1=vT,
                                                   op0=ALU.mult, op1=ALU.add).then_inc(v_added, 1)

            def body(n, g, prev=None):
                for h in range(REP):
                    if prev:
                        add_out(n - 1, *prev, h, (0, 1))
                    if h:
                        cos_q(n + 1, h - 1)
                    else:
                        cos_k(n + 1)
                    if prev:
                        add_out(n - 1, *prev, h, (2, 3))
                    if h == 0:
                        softmax_sum(n)
                    if h == 1:
                        softmax_norm(n)
                cos_q(n + 1, REP - 1)
                scale_v(n + 1, g)
                softmax_max(n + 1)
                context_lo(n)
                softmax_less_max(n + 1)

            cos_k(0)
            scale_v(0, 0)
            for h in range(REP):
                cos_q(0, h)
            softmax_max(0)
            softmax_less_max(0)
            body(0, 0)
            dve.wait_ge(wo_scale_in, 16)
            for b in range(1, BLOCKS):
                dve.wait_ge(acc_zero, b)
                body(b, b // (BLOCKS - 1), (0, b - 1))
            dve.wait_ge(acc_zero, BLOCKS)
            with dve.Fori(1, KV_HEADS - 1) as g:
                body(g * BLOCKS, g, (g - 1, BLOCKS - 1))
                for b in range(1, BLOCKS):
                    body(g * BLOCKS + b, g + b // (BLOCKS - 1), (g, b - 1))
            g = KV_HEADS - 1
            body(g * BLOCKS, g, (g - 1, BLOCKS - 1))
            for b in range(1, BLOCKS - 1):
                body(g * BLOCKS + b, g, (g, b - 1))
            softmax_sum(STEPS - 1)
            softmax_norm(STEPS - 1)
            for h in range(REP):
                add_out(STEPS - 2, g, BLOCKS - 2, h)
            for j, (rows_, src) in enumerate(((slice(RANK, 2 * RANK), sharedB),
                                              (slice(2 * RANK, 2 * RANK + 1), bias_row))):
                dve.wait_ge(lora_sb, j + 1)
                nc.vector.tensor_tensor(outside[1][rows_, :], src, f32(outside[0][rows_, :]),
                                        ALU.subtract).then_inc(shared_ok, 1)
            context_lo(STEPS - 1)
            for h in range(REP):
                add_out(STEPS - 1, g, BLOCKS - 1, h)

            def residual(i):
                dve.wait_ge(xs_in, 16 * i + 16)
                for s in range(2):
                    dve.wait_ge(tx_done, 2 * i + s + 1)
                    nc.vector.tensor_tensor(turned_tile(2 * i + s), ktn(q_bank[2 + s][:, :]),
                                            ktn(x_sb[:, 512 * s:512 * (s + 1)]), ALU.add).then_inc(x1_ok, 1)

            def yT_low(i):
                for s in range(2):
                    dve.wait_ge(yT_hi_ok, 2 * i + s + 1)
                    at = [part.rearrange("p (k t n) -> p k t n", k=KT, t=2)[:, :, s:s + 1, :] for part in yT]
                    nc.vector.tensor_tensor(at[1], ktn(q_bank[2 + s][:, :]), f32(at[0]), ALU.subtract).then_inc(yT_ok, 1)

            def low_low(i):
                dve.wait_ge(low_hi_ok, i + 1)
                nc.vector.tensor_tensor(low[1][0:2 * RANK, :], s_bank[0:2 * RANK, 0:256], f32(low[0][0:2 * RANK, :]),
                                        ALU.subtract).then_inc(low_ok, 1)

            def finish(i):
                for s in range(2):
                    dve.wait_ge(ffn_done, 2 * i + s + 1)
                    at = turned_tile(2 * i + s)
                    nc.vector.tensor_tensor(at, ktn((k_bank, v_bank)[s][:, :]), at, ALU.add).then_inc(result, 1)

            residual(0)
            yT_low(0)
            low_low(0)
            with dve.Fori(0, TILES // 2 - 1) as i:
                residual(i + 1)
                yT_low(i + 1)
                finish(i)
                low_low(i + 1)
            finish(TILES // 2 - 1)

        @block.tensor
        def _(pe):
            def three(dst, terms, start=True, stop=True):
                last = None
                for i, ((lh, ll), (rh, rl)) in enumerate(terms):
                    for j, (l, r) in enumerate(((lh, rh), (ll, rh), (lh, rl))):
                        last = nc.tensor.matmul(dst, l, r, start=start and i == 0 and j == 0,
                                                stop=stop and i == len(terms) - 1 and j == 2)
                return last

            def turn(dst, src):
                for k in range(4):
                    last = nc.tensor.transpose(dst[:, k * P:(k + 1) * P], src[:, k * P:(k + 1) * P], ident)
                return last

            pe.wait_ge(con_in, 16 * (CONV_LOADS + 1))
            nc.tensor.matmul(s_bank[:, 0:64], su["cwT"], su["condT"], start=True, stop=True).then_inc(su_pe, 1)

            def first_layer():
                pe.wait_ge(set_in, 16 * MLP_LOADS)
                nc.tensor.matmul(t_bank[:, 64:128], su["w0"], su["condT"], start=True, stop=True).then_inc(su_pe, 1)

            def second_layer():
                pe.wait_ge(cbias_ok, 4)
                pe.wait_ge(su_act, 1)
                nc.tensor.matmul(s_bank[:, 128:192], su["w1"], su["h1"], start=True, stop=True).then_inc(su_pe, 1)

            def third_layer():
                pe.wait_ge(su_act, 2)
                nc.tensor.matmul(s_bank[0:BATCH, 192:200], su["h2"], su["w2"], start=True, stop=True).then_inc(su_pe, 1)

            def spread():
                pe.wait_ge(su_dve, 6)
                nc.tensor.transpose(s_bank[0:MIX, 256:320], su["att"], ident[0:BATCH, 0:BATCH]).then_inc(su_pe, 1)
                pe.wait_ge(su_dve, 7)
                for k in range(MIX):
                    nc.tensor.matmul(t_bank[:, k * 64:(k + 1) * 64], su["sel"][:, k * 128:(k + 1) * 128], su["attT"],
                                     start=True, stop=True)
                nc.tensor.matmul(s_bank[:, 320:384], su["biask"], su["attT"], start=True, stop=True).then_inc(su_pe, 1)

            pe.wait_ge(convw_ok, 1)

            def convolve(i, r):
                pe.wait_ge(x_in[r], 16 * FOLD * (i + 1))
                for k in range(FOLDS):
                    for b in range(BPT):
                        first = b * XW + k * FOLD
                        last = nc.tensor.matmul(q_bank[r % 2][b * SEQ:(b + 1) * SEQ, :], convw[:, k * 32:(k + 1) * 32],
                                                raw[r][:, first:first + HID], start=k == 0, stop=k == FOLDS - 1)
                last.then_inc(conv_done, 1)

            def turn_h(t, s):
                pe.wait_ge(h_ok, t + 1)
                used(pe, hT_ok, t - 1)
                turn(q_bank[2 + s], h_tile[s]).then_inc(ht_done, 1)

            def four_tiles(i, between=()):
                for r in range(RAW):
                    convolve(i, r)
                    if r or not isinstance(i, int) or i:
                        turn_h(RAW * i + r - 1, (r - 1) % 2)
                    if r < len(between):
                        between[r]()

            four_tiles(0, (first_layer, second_layer, third_layer))
            four_tiles(1, (lambda: None, lambda: None, spread))
            with pe.Fori(2, TILES // RAW) as i:
                four_tiles(i)

            def project(dst, c, blk, slices=range(KT)):
                return three(dst[:, :], [((w_hi[:, c * 512 + k * P:c * 512 + (k + 1) * P],
                                           w_lo[:, c * 512 + k * P:c * 512 + (k + 1) * P]),
                                          (hT(hT_hi, k, blk * BLOCK, BLOCK), hT(hT_lo, k, blk * BLOCK, BLOCK)))
                                         for k in slices], start=slices[0] == 0, stop=slices[-1] == KT - 1)

            def keys(n, blk, g=None, slices=range(KT)):
                if g is not None:
                    pe.wait_ge(w_ready, g * SCALED + C_K + 1)
                used(pe, k_cos, n)
                last = project(k_bank, C_K, blk, slices)
                if slices[-1] == KT - 1:
                    last.then_inc(k_done, 1)

            def queries(h, blk, g=None, slices=range(KT)):
                if g is not None:
                    pe.wait_ge(w_ready, g * SCALED + C_Q + h + 1)
                last = project(q_bank[h], C_Q + h, blk, slices)
                if slices[-1] == KT - 1:
                    last.then_inc(q_done, 1)

            def values(n, blk, k, g=None):
                if g is not None:
                    pe.wait_ge(wv_ready, g + 1)
                if k < 2:
                    used(pe, out_added, PARTS * (n - 1) - k)
                else:
                    pe.wait_ge(v_added, KT * n + k - 1)
                w = w_hi[:, C_V * 512 + k * P:C_V * 512 + (k + 1) * P]
                dst = (s_bank, v_bank)[k % 2][:, :]
                nc.tensor.matmul(dst, w, hT(hT_hi, k, blk * BLOCK, BLOCK), start=True, stop=False)
                nc.tensor.matmul(dst, w, hT(hT_lo, k, blk * BLOCK, BLOCK), start=False, stop=True).then_inc(v_done, 1)

            def output(n, h, slices=range(KT)):
                for k in slices:
                    p = PARTS * n + KT * h + k
                    if h > 0 or k >= 2:
                        pe.wait_ge(out_added, p - 1)
                    w = wo[:, h * HID + k * P:h * HID + (k + 1) * P]
                    dst = (v_bank, s_bank)[k % 2][:, :]
                    nc.tensor.matmul(dst, w, ctx_hi[:, h * BLOCK:(h + 1) * BLOCK], start=True, stop=False)
                    nc.tensor.matmul(dst, w, ctx_lo[:, h * BLOCK:(h + 1) * BLOCK], start=False, stop=True)\
                        .then_inc(out_done, 1)

            def transpose_probs(n):
                pe.wait_ge(sm_step, 5 * n + 5)
                pe.wait_ge(v_ok, n + 1)
                turn(t_bank, prob).then_inc(pt_done, 1)

            def context_of(n, s, tiles=range(TPB), groups=range(BPT)):
                pe.wait_ge(probT_ok, n + 1)
                for t in tiles:
                    for r in groups:
                        rows = slice(32 * r, 32 * r + 32)
                        product = nc.tensor.matmul(q_bank[r][:, t * P:(t + 1) * P], v_sb[s][rows, t * P:(t + 1) * P],
                                                probT[rows, t * P:(t + 1) * P], start=True, stop=True)
                        if t == TPB - 1:
                            product.then_inc(pv_done, 1)

            def scores(n):
                pe.wait_ge(q_roped, REP * (n + 1))
                pe.wait_ge(k_roped, n + 1)
                pe.wait_ge(v_added, KT * n + 3)
                for b in range(BPB):
                    t, r = b // BPT, b % BPT
                    last = nc.tensor.matmul(s_bank[32 * r:32 * r + 32, t * P:(t + 1) * P],
                                            roped_k[:, b * SEQ:(b + 1) * SEQ], roped_q[:, b * P:(b + 1) * P],
                                            start=True, stop=True)
                last.then_inc(scores_done, 1)

            def turn_values(n):
                pe.wait_ge(v_added, KT * (n + 1))
                pe.wait_ge(s_read, n + 1)
                turn(t_bank, vT).then_inc(vt_done, 1)

            def turn_scores(n):
                pe.wait_ge(st_ok, n + 1)
                turn(t_bank, scoreT).then_inc(turned, 1)

            def body(n, b, g, prev=True, first_out=False, last=False):
                nxt = g + 1 if b == BLOCKS - 1 else None
                for h in range(REP):
                    for half in ((0, 1), (2, 3)):
                        if prev:
                            pe.wait_ge(ctx_ok, BPT * (n - 1) + h + 1)
                        queries(h, (b + 1) % BLOCKS, nxt, half)
                        if prev:
                            pe.wait_ge(ctx_ok, BPT * n)
                            if first_out:
                                pe.wait_ge(wo_ready, g + 1)
                            output(n - 1, h, half)
                transpose_probs(n)
                next_keys = ((b + 2) % BLOCKS, g + 1 if b == BLOCKS - 2 else None)
                first, second = (0, 1), (2, 3)
                if not last:
                    keys(n + 2, *next_keys, first)
                values(n + 1, (b + 1) % BLOCKS, 0, nxt)
                values(n + 1, (b + 1) % BLOCKS, 1)
                pe.wait_ge(q_cos, REP * (n + 2))
                context_of(n, b % 2, (0,))
                values(n + 1, (b + 1) % BLOCKS, 2)
                values(n + 1, (b + 1) % BLOCKS, 3)
                context_of(n, b % 2, (1,), first)
                scores(n + 1)
                context_of(n, b % 2, (1,), second)
                context_of(n, b % 2, (2,), first)
                turn_scores(n + 1)
                context_of(n, b % 2, (2,), second)
                context_of(n, b % 2, (3,), (0, 1, 2))
                turn_values(n + 1)
                context_of(n, b % 2, (3,), (3,))
                if not last:
                    keys(n + 2, *next_keys, second)

            turn_h(TILES - 1, 1)
            pe.wait_ge(w_ready, C_K + 1)
            pe.wait_ge(hT_ok, TPB)
            pe.wait_ge(su_dve, 7 + 2 * BPT)
            keys(0, 0)
            for k in range(KT):
                values(0, 0, k, 0 if k == 0 else None)
            for h in range(REP):
                if h == 2:
                    pe.wait_ge(hT_ok, TILES)
                queries(h, 0, 0)
            keys(1, 1)
            scores(0)
            turn_scores(0)
            turn_values(0)
            for b in range(BLOCKS):
                body(b, b, 0, prev=b > 0, first_out=b == 1)
            with pe.Fori(1, KV_HEADS - 1) as g:
                for b in range(BLOCKS):
                    body(g * BLOCKS + b, b, g, first_out=b == 1)
            g = KV_HEADS - 1
            for b in range(BLOCKS - 1):
                body(g * BLOCKS + b, b, g, first_out=b == 1, last=b == BLOCKS - 2)
            def factor_a(k):
                dst = (k_bank, t_bank)[k // 2][:, 256 * (k % 2):256 * (k % 2) + 256]
                for part in range(4):
                    last = nc.tensor.matmul(dst, loraA[:, part * 512 + k * P:part * 512 + (k + 1) * P],
                                            gsel[:, part * 256:(part + 1) * 256], start=part == 0, stop=part == 3)
                if k == KT - 1:
                    last.then_inc(lora_pe, 1)

            def factor_b(j, part):
                last = nc.tensor.matmul(q_bank[j][:, :], gsel[:, part * 256 + j * P:part * 256 + (j + 1) * P],
                                        loraB[:, part * 512:(part + 1) * 512], start=part == 0, stop=part == 3)
                if part == 3:
                    last.then_inc(lora_pe, 1)

            last_block = STEPS - 1
            halves = ((0, 1), (2, 3))
            pe.wait_ge(gsel_ok, 4)
            pe.wait_ge(k_cos, STEPS)
            factor_a(0)
            factor_a(1)
            pe.wait_ge(ctx_ok, BPT * last_block)
            for half in halves:
                output(last_block - 1, 0, half)
            transpose_probs(last_block)
            for part in range(2, 8):
                output(last_block - 1, part // 2, halves[part % 2])
                if part < 2 + TPB:
                    context_of(last_block, last_block % 2, (part - 2,))
            factor_a(2)
            factor_a(3)
            pe.wait_ge(ctx_ok, BPT * STEPS)
            for part in range(8):
                output(last_block, part // 2, halves[part % 2])
                factor_b(part // 4, part % 4)

            def turn_back(i):
                for s in range(2):
                    pe.wait_ge(at_ok, 2 * i + s + 1)
                    used(pe, yT_ok, 2 * i)
                    turn(q_bank[2 + s], at_sb[s]).then_inc(tx_done, 1)

            def mix(i):
                for s in range(2):
                    pe.wait_ge(bd_ok, 2 * i + s + 1)
                    pe.wait_ge(x1_ok, 2 * i + s + 1)
                    nc.tensor.matmul(q_bank[s][:, :], mixbd[s], turned_tile(2 * i + s),
                                     start=True, stop=True).then_inc(y_done, 1)

            def transpose_y(i):
                for s in range(2):
                    pe.wait_ge(y_ok, 2 * i + s + 1)
                    turn(q_bank[2 + s], y_sb[s]).then_inc(yt_done, 1)

            def low_rank(i):
                pe.wait_ge(yT_ok, 2 * i + 2)
                pe.wait_ge(inside_ok, i + 1)
                three(s_bank[0:2 * RANK, 0:256],
                      [(tuple(part[:, k * 2 * RANK:(k + 1) * 2 * RANK] for part in inside),
                        tuple(part[:, k * 256:(k + 1) * 256] for part in yT))
                       for k in range(KT)]).then_inc(low_done, 1)

            def times_kernel(i, s, slices=range(KT)):
                used(pe, result, 2 * i)
                last = three((k_bank, v_bank)[s][:, :],
                             [(tuple(part[:, k * 256 + s * P:k * 256 + (s + 1) * P] for part in yT),
                               tuple(part[:, k * 512:(k + 1) * 512] for part in kern_parts)) for k in slices],
                             start=slices[0] == 0, stop=False)
                if slices[-1] == KT - 1:
                    last.then_inc(kern_used, 1)

            def low_rank_out(i):
                pe.wait_ge(low_ok, i + 1)
                pe.wait_ge(outside_ok, i + 1)
                for s in range(2):
                    three((k_bank, v_bank)[s][:, :],
                          [(tuple(part[:, s * P:(s + 1) * P] for part in low), outside)], start=False).then_inc(ffn_done, 1)

            turn_back(0)
            pe.wait_ge(kern_ok, 1)
            pe.wait_ge(shared_ok, 2)
            pe.wait_ge(out_added, PARTS * STEPS)
            pe.wait_ge(lora_sb, 2 + 2 * KT + LGROUPS)
            mix(0)
            transpose_y(0)
            low_rank(0)

            def ffn_body(i):
                turn_back(i + 1)
                times_kernel(i, 0)
                mix(i + 1)
                times_kernel(i, 1, (0, 1))
                transpose_y(i + 1)
                times_kernel(i, 1, (2, 3))
                low_rank_out(i)
                low_rank(i + 1)

            ffn_body(0)
            with pe.Fori(1, TILES // 2 - 1) as i:
                ffn_body(i)
            i = TILES // 2 - 1
            times_kernel(i, 0)
            times_kernel(i, 1)
            low_rank_out(i)


def constants():
    import numpy as np
    con = np.zeros((P, CON_N), np.float32)
    p = np.arange(P)
    inv = (1.0 / np.float32(10000.0) ** (np.arange(0, HEAD, 2, dtype=np.float32) / np.float32(HEAD))).astype(np.float32)
    freq = np.arange(SEQ, dtype=np.float32)[:, None] * inv
    con[:, COS:COS + SEQ] = np.concatenate([np.cos(freq), np.cos(freq)], 1).T
    con[:, SIN:SIN + SEQ] = np.concatenate([-np.sin(freq), np.sin(freq)], 1).T
    big = np.finfo(np.float32)
    con[:, LIM:LIM + SEQ] = np.where(np.arange(SEQ)[None] <= (p % SEQ)[:, None], big.max, big.min)
    con[:, IDN:IDN + P] = np.eye(P, dtype=np.float32)
    con[:, BDG:BDG + 4] = (p[:, None] % 32 // 8 == np.arange(4)[None])
    con[:, BD32:BD32 + BPT] = (p[:, None] // 32 == np.arange(BPT)[None])
    con[:, ID32:ID32 + 32] = (p[:, None] % 32 == np.arange(32)[None])
    sel = np.zeros((MIX, MIX, P), np.float32)
    for k in range(MIX):
        sel[k, k] = 1.0
    return con, sel.reshape(MIX, MIX * P)


def kernel(**inputs):
    import numpy as np
    import concourse.bacc as bacc
    from concourse import mybir as mb
    from concourse.bass_utils import run_bass_kernel_spmd

    i = {k: np.asarray(v) for k, v in inputs.items()}
    c = np.ascontiguousarray

    def proj(w):
        return w.reshape(KT, P, -1, P).transpose(2, 1, 0, 3).reshape(-1, P, 512)

    def srow(w):
        return w.reshape(KT, -1, P).transpose(1, 0, 2).reshape(-1, 512)

    def group(k, q, v):
        return c(np.concatenate([k[:, None], q.reshape(KV_HEADS, REP, *q.shape[1:]), v[:, None]], axis=1))

    taps = np.zeros((FOLDS * FOLD, 32, 8), i["L0_cond_weight"].dtype)
    taps[:TAPS] = i["L0_cond_weight"].reshape(4, 8, 8, TAPS).transpose(3, 0, 2, 1).reshape(TAPS, 32, 8)
    taps = taps.reshape(FOLDS, FOLD * 32, 8).transpose(1, 0, 2)

    con, sel = constants()
    arrays = {
        "con": con, "sel": sel,
        "x": c(i["x"].reshape(TILES, P, HID)),
        "condT": c(i["cond_128"].T),
        "fb": c(np.tile(i["fside_S_0"], BPT).reshape(P, 1)),
        "taps": c(taps.reshape(P, FOLDS * 8)),
        "cwT": c(np.tile(i["L0_cond_c_weight"].T, (1, BPT))),
        "w0": c(i["L0_cond2_W0"]), "w1": c(i["L0_cond2_W1"]), "w2": c(i["L0_cond2_W2"]),
        "b0": c(i["L0_cond2_b0"].reshape(P, 1)), "b1": c(i["L0_cond2_b1"].reshape(P, 1)),
        "b2": c(i["L0_cond2_b2"].reshape(1, MIX)),
        "biask": c(np.tile(i["L0_cond2_bias_k"], (1, BPT))),
        "mixk": c(np.tile(i["L0_cond2_weight"][..., 0].transpose(2, 0, 1).reshape(32, MIX * 32), (BPT, 1))),
        "qw": group(proj(i["L0_attn_qw_k"]), proj(i["L0_attn_qw_q"]), proj(i["L0_attn_qw_v"])),
        "scales": group(srow(i["L0_attn_scales_k"]), srow(i["L0_attn_scales_q"]), srow(i["L0_attn_scales_v"])),
        "v_scale": c(i["L0_attn_scales_v"].reshape(KT, KV_HEADS, P).transpose(2, 1, 0).reshape(P, -1)),
        "wo": c(i["L0_attn_qw_o"].reshape(KV_HEADS, REP, P, HID).transpose(0, 2, 1, 3).reshape(KV_HEADS, P, REP * HID)),
        "wo_scale": c(i["L0_attn_scales_o"].reshape(KV_HEADS * REP, KT, P).transpose(2, 0, 1).reshape(P, -1)),
        "kern": c(i["L0_ffn_kernel"].reshape(KT, P, 512).transpose(1, 0, 2)),
        "fbias": c(i["L0_ffn_bias"].reshape(1, HID)),
        "loraA": c(i["L0_ffn_lora_A"].reshape(4, P, 512).transpose(1, 0, 2)),
        "loraB": c(i["L0_ffn_lora_B"].transpose(0, 2, 1).reshape(4, P, 512).transpose(1, 0, 2)),
        "gateT": c(i["L0_ffn_gate"].T.reshape(4, 4, LGROUPS).transpose(1, 0, 2).reshape(4, 32)),
        "sharedA": c(i["L0_ffn_lora_A_shared"].T.reshape(KT, P, RANK).transpose(1, 0, 2).reshape(P, KT * RANK)),
        "sharedB": c(i["L0_ffn_lora_B_shared"].T),
    }
    nc = bacc.Bacc("TRN2", target_bir_lowering=False, num_devices=1)
    aps = {k: nc.dram_tensor(f"in_{k}", v.shape, mb.dt.from_np(v.dtype), kind="ExternalInput").ap()
           for k, v in arrays.items()}
    out = nc.dram_tensor("out_x", (TILES, P, HID), mb.dt.from_np(np.dtype("float32")), kind="ExternalOutput").ap()
    build(nc, aps, out)
    r = run_bass_kernel_spmd(nc, [{f"in_{k}": v for k, v in arrays.items()}], core_ids=[0])
    return r.results[0]["out_x"].reshape(BATCH, SEQ, HID)
```
